# Optimizing a Trainium2 kernel written in Bass

```python
import numpy as np
import jax
import jax.numpy as jnp

def _softmax(x, axis=-1):
    return jax.nn.softmax(x, axis=axis)

def _gelu(x):
    return jax.nn.gelu(x, approximate=True)

def _silu(x):
    return jax.nn.silu(x)

def _sigmoid(x):
    return jax.nn.sigmoid(x)

def _layernorm(x, axis=-1, eps=1e-05):
    m = jnp.mean(x, axis=axis, keepdims=True)
    v = jnp.var(x, axis=axis, keepdims=True)
    return (x - m) / jnp.sqrt(v + eps)

def _scatter_add(tgt, idx, src, axis=0):
    return tgt.at[idx].add(src)

def _segment_sum(src, seg, n):
    return jax.ops.segment_sum(src, seg, n)
kernel_name = 'mk_prb_d1_jaxref_r4_a2e899'

def setup_inputs(seed: int=0):
    np.random.seed(seed)
    _w = jnp.asarray

    def _L0_attn_setup():
        import jax, jax.numpy as jnp
        import numpy as np
        B, S, D, H = (2, 512, 256, 16)
        DEPTH = D // H
        EPS = 1e-06

        def _split_heads(t):
            b, s, _ = t.shape
            return t.reshape(b, s, H, DEPTH).transpose(0, 2, 1, 3)
        key = jax.random.key(seed)
        ks = jax.random.split(key, 6)
        glorot = lambda k: jax.random.uniform(k, (D, D), jnp.float32, -1.0, 1.0) * np.sqrt(6.0 / (D + D))
        return {'x': jax.random.normal(ks[0], (B, S, D), jnp.float32), 'Wq': glorot(ks[1]), 'bq': jnp.zeros((D,), jnp.float32), 'Wk': glorot(ks[2]), 'bk': jnp.zeros((D,), jnp.float32), 'Wv': glorot(ks[3]), 'bv': jnp.zeros((D,), jnp.float32), 'Wo': glorot(ks[4]), 'bo': jnp.zeros((D,), jnp.float32), 'gamma': jnp.ones((D,), jnp.float32), 'beta': jnp.zeros((D,), jnp.float32)}
    _L0_attn_in = _L0_attn_setup()

    def _L0_ffn_setup():
        import jax, jax.numpy as jnp
        import numpy as np
        GROUP = 16
        EPS = 1e-05

        def _dequant(q, scale):
            w = q.astype(jnp.float32) / 7.5 - 1.0
            return w * jnp.repeat(scale, GROUP, axis=1)

        def _qlora_linear(x, q, scale, bias, la, lb):
            w = _dequant(q, scale)
            base = jnp.einsum('btd,od->bto', x, w) + bias
            lora = jnp.einsum('btr,or->bto', jnp.einsum('btd,rd->btr', x, la), lb)
            return base + lora

        def _layernorm(x, g, b):
            mu = jnp.mean(x, axis=-1, keepdims=True)
            var = jnp.mean(jnp.square(x - mu), axis=-1, keepdims=True)
            return (x - mu) * jax.lax.rsqrt(var + EPS) * g + b
        key = jax.random.key(seed)
        ks = jax.random.split(key, 6)
        D, R, B, T = (256, 32, 8, 1024)
        x = jax.random.normal(ks[0], (B, T, D), dtype=jnp.float32)
        qweights = jax.random.randint(ks[1], (6, D, D), 0, 16, dtype=jnp.int32)
        scales = jax.random.uniform(ks[2], (6, D, D // GROUP), dtype=jnp.float32)
        biases = jax.random.normal(ks[3], (6, D), dtype=jnp.float32) * 0.02
        lora_a = jax.random.normal(ks[4], (6, R, D), dtype=jnp.float32) * 0.02
        lora_b = jax.random.normal(ks[5], (6, D, R), dtype=jnp.float32) * 0.02
        ln_gamma = jnp.ones((3, D), dtype=jnp.float32)
        ln_beta = jnp.zeros((3, D), dtype=jnp.float32)
        return {'x': x, 'qweights': qweights, 'scales': scales, 'biases': biases, 'lora_a': lora_a, 'lora_b': lora_b, 'ln_gamma': ln_gamma, 'ln_beta': ln_beta}
    _L0_ffn_in = _L0_ffn_setup()
    _d = {'L0_attn_x': _L0_attn_in['x'], 'L0_attn_Wq': _L0_attn_in['Wq'], 'L0_attn_bq': _L0_attn_in['bq'], 'L0_attn_Wk': _L0_attn_in['Wk'], 'L0_attn_bk': _L0_attn_in['bk'], 'L0_attn_Wv': _L0_attn_in['Wv'], 'L0_attn_bv': _L0_attn_in['bv'], 'L0_attn_Wo': _L0_attn_in['Wo'], 'L0_attn_bo': _L0_attn_in['bo'], 'L0_attn_gamma': _L0_attn_in['gamma'], 'L0_attn_beta': _L0_attn_in['beta'], 'L0_ffn_qweights': _L0_ffn_in['qweights'], 'L0_ffn_scales': _L0_ffn_in['scales'], 'L0_ffn_biases': _L0_ffn_in['biases'], 'L0_ffn_lora_a': _L0_ffn_in['lora_a'], 'L0_ffn_lora_b': _L0_ffn_in['lora_b'], 'L0_ffn_ln_gamma': _L0_ffn_in['ln_gamma'], 'L0_ffn_ln_beta': _L0_ffn_in['ln_beta']}
    _x0 = _d['L0_attn_x']
    _d['L0_attn_x'] = jax.random.normal(jax.random.fold_in(jax.random.key(seed), 1), (8, 1024, 256), dtype=_x0.dtype)
    del _x0
    return _d

def reference(L0_attn_x, L0_attn_Wq, L0_attn_bq, L0_attn_Wk, L0_attn_bk, L0_attn_Wv, L0_attn_bv, L0_attn_Wo, L0_attn_bo, L0_attn_gamma, L0_attn_beta, L0_ffn_qweights, L0_ffn_scales, L0_ffn_biases, L0_ffn_lora_a, L0_ffn_lora_b, L0_ffn_ln_gamma, L0_ffn_ln_beta):

    def _L0_attn_ref(x, Wq, bq, Wk, bk, Wv, bv, Wo, bo, gamma, beta):
        import jax, jax.numpy as jnp
        import numpy as np
        B, S, D, H = (2, 512, 256, 16)
        DEPTH = D // H
        EPS = 1e-06

        def _split_heads(t):
            b, s, _ = t.shape
            return t.reshape(b, s, H, DEPTH).transpose(0, 2, 1, 3)
        b, s, d = x.shape
        q = _split_heads(x @ Wq + bq)
        k = _split_heads(x @ Wk + bk)
        v = _split_heads(x @ Wv + bv)
        q = jax.nn.elu(q) + 1.0
        k = jax.nn.elu(k) + 1.0
        k = k / jnp.sqrt(jnp.sum(k * k, axis=-1, keepdims=True) + EPS)
        scores = jnp.einsum('bhqd,bhkd->bhqk', q, k)
        attn = jnp.einsum('bhqk,bhkd->bhqd', scores, v)
        attn = attn.transpose(0, 2, 1, 3).reshape(b, s, d)
        out = attn @ Wo + bo
        y = x + out
        mu = jnp.mean(y, axis=-1, keepdims=True)
        var = jnp.mean(jnp.square(y - mu), axis=-1, keepdims=True)
        return (y - mu) / jnp.sqrt(var + EPS) * gamma + beta

    def _L0_ffn_ref(x, qweights, scales, biases, lora_a, lora_b, ln_gamma, ln_beta):
        import jax, jax.numpy as jnp
        import numpy as np
        GROUP = 16
        EPS = 1e-05

        def _dequant(q, scale):
            w = q.astype(jnp.float32) / 7.5 - 1.0
            return w * jnp.repeat(scale, GROUP, axis=1)

        def _qlora_linear(x, q, scale, bias, la, lb):
            w = _dequant(q, scale)
            base = jnp.einsum('btd,od->bto', x, w) + bias
            lora = jnp.einsum('btr,or->bto', jnp.einsum('btd,rd->btr', x, la), lb)
            return base + lora

        def _layernorm(x, g, b):
            mu = jnp.mean(x, axis=-1, keepdims=True)
            var = jnp.mean(jnp.square(x - mu), axis=-1, keepdims=True)
            return (x - mu) * jax.lax.rsqrt(var + EPS) * g + b
        h = x
        for blk in range(3):
            i0, i1 = (2 * blk, 2 * blk + 1)
            y = _qlora_linear(h, qweights[i0], scales[i0], biases[i0], lora_a[i0], lora_b[i0])
            y = _layernorm(y, ln_gamma[blk], ln_beta[blk])
            y = jax.nn.gelu(y, approximate=False)
            y = _qlora_linear(y, qweights[i1], scales[i1], biases[i1], lora_a[i1], lora_b[i1])
            h = y + h
        return h
    x = L0_attn_x
    xn = _layernorm(x, axis=-1)
    x = x + _L0_attn_ref(xn, L0_attn_Wq, L0_attn_bq, L0_attn_Wk, L0_attn_bk, L0_attn_Wv, L0_attn_bv, L0_attn_Wo, L0_attn_bo, L0_attn_gamma, L0_attn_beta) + _L0_ffn_ref(xn, L0_ffn_qweights, L0_ffn_scales, L0_ffn_biases, L0_ffn_lora_a, L0_ffn_lora_b, L0_ffn_ln_gamma, L0_ffn_ln_beta)
    return x

_drawn_inputs = setup_inputs


def setup_inputs(seed=0):
    import zlib

    import numpy as np

    out = dict(_drawn_inputs(seed))
    spreads = {'L0_attn_bq': (0.0, 2.0),
     'L0_attn_bk': (0.0, 2.0),
     'L0_attn_bv': (0.0, 0.1),
     'L0_attn_bo': (0.0, 2.0),
     'L0_attn_gamma': (1.0, 0.535),
     'L0_attn_beta': (0.0, 0.622),
     'L0_ffn_ln_gamma': (1.0, 0.2),
     'L0_ffn_ln_beta': (0.0, 0.1)}
    factors = {'L0_attn_Wk': 5.183,
     'L0_ffn_biases': 7.889,
     'L0_ffn_lora_a': 4.828,
     'L0_ffn_lora_b': 4.711}
    for name, (base, spread) in spreads.items():
        noise = np.random.default_rng([zlib.crc32(name.encode()), seed]).standard_normal(out[name].shape)
        drawn = base * np.exp(spread * noise) if base else spread * noise
        out[name] = jnp.asarray(drawn.astype(out[name].dtype))
    for name, factor in factors.items():
        out[name] = (out[name] * factor).astype(out[name].dtype)
    return out
```

```python
from contextlib import ExitStack

import concourse.bass as bass
from concourse import mybir

ALU = mybir.AluOpType
ACT = mybir.ActivationFunctionType
F32 = mybir.dt.float32
I32 = mybir.dt.int32
AX_X = mybir.AxisListType.X

P = 128
BANK = 512
NT = 8
HT = NT // 2
NBLK = 3
DEPTH = 16
GROUP = 16
EPS_LN = 1e-5
EPS_ATTN = 1e-6

def bank_uses(last):
    uses = [("var", 0, 0), ("kv", 0), ("kv", 1), ("rs", 0, 0), ("var", 1, 0), ("kv", 2), ("kv", 3), ("rs", 1, 0)]
    uses += [("kv", 4), ("var", 0, 1), ("kv", 5), ("kv", 6), ("rs", 0, 1), ("var", 1, 1), ("kv", 7),
             ("q", 0, 0), ("q", 0, 1), ("rs", 1, 1)]
    uses += [("q", 1, 0), ("q", 1, 1), ("var", 0, 2), ("rs", 0, 2), ("out", 0), ("var", 1, 2), ("out", 1),
             ("rs", 1, 2), ("out", 2), ("out", 3)]
    if not last:
        uses += [("xt", 0, 0), ("xt", 0, 1), ("xt", 1, 0), ("xt", 1, 1)]
    uses += [("fin", 0), ("fin", 1), ("fin", 2), ("fin", 3)]
    return uses


USES = len(bank_uses(False))
NROT = 3
AHEAD = 4
assert USES % NROT == 0


def rotating(i, use, last):
    n = AHEAD + bank_uses(last).index(use)
    return n % NROT, i * (USES // NROT) + n // NROT


def nth(i, per, n):
    return i * per + (n + 1)


def block_kernel(nc: bass.Bass, x, Wq, bq, Wk, bk, Wv, bv, Wo, bo, gamma, beta,
                 qweights, scales, biases, lora_a, lora_b, ln_gamma, ln_beta, out):
    NB, S, D = x.shape
    NL = qweights.shape[0]
    R = lora_a.shape[1]
    NC = D // P
    NG = D // GROUP
    NH = D // DEPTH
    assert S == NT * P and NC == 2 and NL == 2 * NBLK and D == 256

    x_rows = x.rearrange("b (p t) d -> b p t d", t=NT)
    out_rows = out.rearrange("b (p t) d -> b p t d", t=NT)

    ctx = ExitStack()
    with ctx:
        def sb(name, shape, dt=F32):
            return ctx.enter_context(nc.sbuf_tensor(name, shape, dt))

        def sem(name):
            return ctx.enter_context(nc.semaphore(name))

        q_int = sb("q_int", [P, NL, NC, D], I32)
        sc = sb("sc", [P, NL, NC, NG])
        la = sb("la", [R, NL, D])
        lb = sb("lb", [P, NL, NC, R])
        lbT = sb("lbT", [R, NL * NC * P])
        w_od = sb("w_od", [P, 2, NC * D])
        WT = sb("WT", [P, NL, NC, D])
        Wqs = sb("Wqs", [P, NC, D])
        Wkv = sb("Wkv", [P, NC, 2 * D])
        Wos = sb("Wos", [P, NC, D])
        ident = sb("ident", [P, P])
        head_mask = sb("head_mask", [P, P])
        mean_w = sb("mean_w", [P, P])
        ones = sb("ones", [P, 1])
        neg1 = sb("neg1", [P, 1])
        neghalf = sb("neghalf", [P, HT])
        kvb = sb("kvb", [P, 2 * D])
        bo_r = sb("bo_r", [P, D])
        gamma_r = sb("gamma_r", [P, D])
        beta_r = sb("beta_r", [P, D])
        b1_r = sb("b1_r", [P, NBLK, D])
        fb = sb("fb", [P, NL, NC])
        lng = sb("lng", [P, NBLK, NC])
        lnb = sb("lnb", [P, NBLK, NC])
        bqc = sb("bqc", [P, NC])
        bq1 = sb("bq1", [P, NC])
        b1c = sb("b1c", [P, NBLK, NC])
        b1m = sb("b1m", [P, NBLK])
        wmean = sb("wmean", [P, 2, NC])
        X = sb("X", [P, NT, D])
        XN = sb("XN", [P, NT, D])
        XNB = sb("XNB", [P, NT, D])
        RES = sb("RES", [P, NT, D])
        O = sb("O", [P, NT, D])
        xT = [sb(f"xT{c}", [P, S]) for c in range(NC)]
        hT = [sb(f"hT{c}", [P, S]) for c in range(NC)]
        qT = [sb(f"qT{c}", [P, S]) for c in range(NC)]
        st1 = sb("st1", [P, NT, 6])
        mv1 = sb("mv1", [P, NT, 2])
        ve1 = sb("ve1", [P, NT])
        rs1 = sb("rs1", [P, NT])
        st2 = sb("st2", [P, NT, 6])
        mv2 = sb("mv2", [P, NT, 2])
        ve2 = sb("ve2", [P, NT])
        rs2 = sb("rs2", [P, NT])
        sq = sb("sq", [P, 2, NC, BANK])
        sqs = sb("sqs", [P, 2, BANK])
        vef = sb("vef", [P, 2, HT])
        rsf = sb("rsf", [P, 2, HT])
        rb = sb("rb", [P, 2, BANK])
        yn = sb("yn", [P, 2, NC, BANK])
        g = sb("g", [P, 2, NC, BANK])
        KV = sb("KV", [P, HT, 2 * D])
        E = sb("E", [P, HT, D])
        K = sb("K", [P, HT, D])
        KS = sb("KS", [P, HT, D])
        KH = sb("KH", [P, HT, D])
        ss = sb("ss", [P, HT, NH])
        sse = sb("sse", [P, HT * NH])
        lnk = sb("lnk", [P, HT * NH])
        r0 = sb("r0", [P, HT * NH])
        ra = sb("ra", [P, HT * NH])
        rc = sb("rc", [P, HT * NH])
        rk = sb("rk", [P, HT, NH])
        eq = sb("eq", [P, NC, BANK])
        BD = sb("BD", [P, NC * P])
        M = sb("M", [P, NC, D])
        Y = sb("Y", [P, 2, 2, D])
        Z = sb("Z", [P, 4, D])

        bank = [ctx.enter_context(nc.psum_tensor(f"bank{n}", [P, BANK], F32)) for n in range(8)]
        FB = [bank[0:2], bank[2:4]]
        AB = bank[4]
        RB = bank[5:8]

        w_q, w_sc, w_la, w_lb, w_qkvo, w_row, w_col = (
            sem(n) for n in ("w_q", "w_sc", "w_la", "w_lb", "w_qkvo", "w_row", "w_col"))
        consts = sem("consts")
        consts_step = sem("consts_step")
        dve_prep = sem("dve_prep")
        lbT_full = sem("lbT_full")
        lbT_ready = sem("lbT_ready")
        lora_full = sem("lora_full")
        w_od_ready = sem("w_od_ready")
        wT_full = sem("wT_full")
        wT_centred = sem("wT_centred")
        wT_copied = sem("wT_copied")
        vecs_ready = sem("vecs_ready")
        x_loaded = [sem(f"x_loaded{h}") for h in range(2)]
        x_based = sem("x_based")
        xn_based = sem("xn_based")
        ln1_stats, ln1_mean, ln1_var, ln1_rstd, xn_ready = (
            sem(n) for n in ("ln1_stats", "ln1_mean", "ln1_var", "ln1_rstd", "xn_ready"))
        stats_seen = sem("stats_seen")
        xT_ready = sem("xT_ready")
        rot_full = [sem(f"rot_full{n}") for n in range(NROT)]
        ffn_full = [[sem(f"ffn_full{h}{m}") for m in range(NC)] for h in range(2)]
        m_full = sem("m_full")
        sq_ready, sqs_ready, fvar_ready, frstd_ready, rb_ready, yn_ready, g_ready, h_ready = (
            [sem(f"{n}{h}") for h in range(2)]
            for n in ("sq_ready", "sqs_ready", "fvar_ready", "frstd_ready", "rb_ready", "yn_ready", "g_ready",
                      "h_ready"))
        kv_ready, e_ready, k_ready, ks_ready, ss_ready, sse_ready, lnk_ready, r0_ready, ra_ready, rc_ready, rk_ready, \
            kh_ready, kvt_done = (sem(n) for n in (
                "kv_ready", "e_ready", "k_ready", "ks_ready", "ss_ready", "sse_ready", "lnk_ready", "r0_ready",
                "ra_ready", "rc_ready", "rk_ready", "kh_ready", "kvt_done"))
        eq_ready, eq_min, q_ready, bd_ready, m_ready = (
            sem(n) for n in ("eq_ready", "eq_min", "q_ready", "bd_ready", "m_ready"))
        y_ready, ln2_stats, ln2_mean, ln2_var, ln2_rstd, z_ready, res_ready = (
            sem(n) for n in ("y_ready", "ln2_stats", "ln2_mean", "ln2_var", "ln2_rstd", "z_ready", "res_ready"))
        o_ready = sem("o_ready")
        stored = [sem(f"stored{h}") for h in range(2)]

        def half(h):
            return slice(h * BANK, (h + 1) * BANK)

        def batches(engine, body):
            body(0, True, False)
            with engine.Fori(1, NB - 1) as i:
                body(i, False, False)
            body(NB - 1, False, True)

        block = ctx.enter_context(nc.Block())

        @block.sync
        def _(sp):
            def load_x(b, h):
                sp.dma_start(X[:, h * HT:(h + 1) * HT, :],
                             x_rows[bass.ds(b, 1), :, h * HT:(h + 1) * HT, :].rearrange("o p t d -> (o p) t d")
                             ).then_inc(x_loaded[h], 16)

            load_x(0, 0)
            load_x(0, 1)
            for c, (w, dst) in enumerate(((Wk, Wkv[:, :, 0:D]), (Wv, Wkv[:, :, D:]), (Wq, Wqs[:]), (Wo, Wos[:]))):
                sp.dma_start(dst, w.rearrange("(c p) n -> p c n", p=P)).then_inc(w_qkvo, 16)
            sp.dma_start(la[:], lora_a.rearrange("l r d -> r l d")).then_inc(w_la, 16)

            def body(i, first, last):
                for h in range(2):
                    if not last:
                        sp.wait_ge(xn_based, nth(i, 2, h))
                        load_x(i + 1, h)
                for h in range(2):
                    sp.wait_ge(o_ready, nth(i, NT // 2, 2 * h + 1))
                    sp.dma_start(out_rows[bass.ds(i, 1), :, h * HT:(h + 1) * HT, :].rearrange("o p t d -> (o p) t d"),
                                 O[:, h * HT:(h + 1) * HT, :]).then_inc(stored[h], 16)

            batches(sp, body)
            for h in range(2):
                sp.wait_ge(stored[h], 16 * NB)

        @block.gpsimd
        def _(pool):
            pool.memset(ident[:], 0.0).then_inc(consts_step, 1)
            pool.memset(head_mask[:], 1.0).then_inc(consts_step, 1)
            pool.memset(mean_w[:], 1.0 / D).then_inc(consts, 1)
            pool.memset(ones[:], 1.0).then_inc(consts, 1)
            pool.memset(neg1[:], -1.0).then_inc(consts, 1)
            pool.memset(neghalf[:], -0.5).then_inc(consts, 1)
            pool.wait_ge(consts_step, 2)
            pool.affine_select(out=ident[:], in_=ident[:], compare_op=ALU.not_equal, fill=1.0,
                               base=0, pattern=[[-1, P]], channel_multiplier=1).then_inc(consts, 1)
            heads = head_mask[:].rearrange("p (h d) -> p h d", d=DEPTH)
            pool.affine_select(out=heads, in_=heads, compare_op=ALU.is_ge, fill=0.0, base=0,
                               pattern=[[-DEPTH, P // DEPTH], [0, DEPTH]], channel_multiplier=1
                               ).then_inc(consts_step, 1)
            pool.wait_ge(consts_step, 3)
            pool.affine_select(out=heads, in_=heads, compare_op=ALU.is_ge, fill=0.0, base=DEPTH - 1,
                               pattern=[[DEPTH, P // DEPTH], [0, DEPTH]], channel_multiplier=-1).then_inc(consts, 1)

            def rstd(dst, var, n):
                return pool.tensor_tensor(dst, var, neghalf[:, 0:n], ALU.pow)

            def ln1_root(b, h):
                pool.wait_ge(ln1_var, nth(b, 2, h))
                rstd(rs1[:, h * HT:(h + 1) * HT], ve1[:, h * HT:(h + 1) * HT], HT).then_inc(ln1_rstd, 1)

            def base_x(b, h, first):
                pool.wait_ge(x_loaded[h], 16 * b + 16)
                if not first:
                    pool.wait_ge(o_ready, nth(b - 1, NT // 2, 2 * h + 1))
                pool.tensor_tensor(RES[:, h * HT:(h + 1) * HT, :], X[:, h * HT:(h + 1) * HT, :],
                                   beta_r[:].unsqueeze(1).broadcast_to([P, HT, D]), ALU.add).then_inc(x_based, 1)

            def base_xn(b, h, first):
                pool.wait_ge(xn_ready, nth(b, NT, h * HT + HT - 1))
                if not first:
                    pool.wait_ge(y_ready, nth(b - 1, NT // 2, 2 * h + 1))
                pool.tensor_tensor(XNB[:, h * HT:(h + 1) * HT, :], XN[:, h * HT:(h + 1) * HT, :],
                                   bo_r[:].unsqueeze(1).broadcast_to([P, HT, D]), ALU.add).then_inc(xn_based, 1)

            def add_squares(i, h, j):
                pool.wait_ge(sq_ready[h], nth(i, NBLK * NC, j * NC + NC - 1))
                pool.tensor_tensor(sqs[:, h, :], sq[:, h, 0, :], sq[:, h, 1, :], ALU.add).then_inc(sqs_ready[h], 1)

            def ffn_root(i, h, j):
                pool.wait_ge(fvar_ready[h], nth(i, NBLK, j))
                rstd(rsf[:, h, :], vef[:, h, :], HT).then_inc(frstd_ready[h], 1)

            def ln2_root(i, p):
                pool.wait_ge(ln2_var, nth(i, NT // 2, p))
                rstd(rs2[:, 2 * p:2 * p + 2], ve2[:, 2 * p:2 * p + 2], 2).then_inc(ln2_rstd, 1)

            for h in range(2):
                ln1_root(0, h)
            pool.wait_ge(w_row, 96)
            pool.wait_ge(consts, 6)

            def body(i, first, last):
                add_squares(i, 0, 0)
                add_squares(i, 1, 0)
                ffn_root(i, 0, 0)
                base_x(i, 0, first)
                ffn_root(i, 1, 0)
                base_x(i, 1, first)
                base_xn(i, 0, first)
                base_xn(i, 1, first)
                for j in range(1, NBLK):
                    add_squares(i, 0, j)
                    add_squares(i, 1, j)
                    ffn_root(i, 0, j)
                    if j == 2:
                        ln2_root(i, 0)
                    ffn_root(i, 1, j)
                for p in range(1, NT // 2):
                    ln2_root(i, p)
                if not last:
                    for h in range(2):
                        ln1_root(i + 1, h)

            batches(pool, body)

        @block.scalar
        def _(act):
            act.dma_start(q_int[:], qweights.rearrange("l (c p) d -> p l c d", p=P)).then_inc(w_q, 16)
            act.dma_start(sc[:], scales.rearrange("l (c p) g -> p l c g", p=P)).then_inc(w_sc, 16)
            act.dma_start(lb[:], lora_b.rearrange("l (c p) r -> p l c r", p=P)).then_inc(w_lb, 16)
            for dst, src in ((kvb[:, 0:D], bk), (kvb[:, D:], bv), (bo_r[:], bo), (gamma_r[:], gamma), (beta_r[:], beta)):
                act.dma_start(dst, src.unsqueeze(0).broadcast_to([P, D])).then_inc(w_row, 16)
            act.dma_start(b1_r[:], biases.rearrange("(j two) d -> two j d", two=2)[0:1]
                          .broadcast_to([P, NBLK, D])).then_inc(w_row, 16)
            with nc.allow_non_contiguous_dma(reason="short vectors, feature on the partition"):
                act.dma_start(fb[:], biases.rearrange("l (c p) -> p l c", p=P)).then_inc(w_col, 16)
                act.dma_start(lng[:], ln_gamma.rearrange("l (c p) -> p l c", p=P)).then_inc(w_col, 16)
                act.dma_start(lnb[:], ln_beta.rearrange("l (c p) -> p l c", p=P)).then_inc(w_col, 16)
                act.dma_start(bqc[:], bq.rearrange("(c p) -> p c", p=P)).then_inc(w_col, 16)

            def xt_copy(b, h, c, last, ahead=False):
                r, n = (h * NC + c) % NROT, (h * NC + c) // NROT
                if not ahead:
                    r, n = rotating(b - 1, ("xt", h, c), last)
                act.wait_ge(rot_full[r], n + 1)
                act.activation(xT[c][:, half(h)], RB[r][:], ACT.Copy).then_inc(xT_ready, 1)

            def squares(i, h, j):
                for m in range(NC):
                    act.wait_ge(ffn_full[h][m], nth(i, 2 * NBLK, 2 * j))
                    act.activation(sq[:, h, m, :], FB[h][m][:], ACT.Square, bias=b1c[:, j, m:m + 1]
                                   ).then_inc(sq_ready[h], 1)

            def rb_copy(i, h, j, last):
                r, n = rotating(i, ("rs", h, j), last)
                act.wait_ge(rot_full[r], n + 1)
                act.activation(rb[:, h, :], RB[r][:], ACT.Copy).then_inc(rb_ready[h], 1)

            def gelus(i, h, j):
                for m in range(NC):
                    act.wait_ge(yn_ready[h], nth(i, NBLK * NC, j * NC + m))
                    act.activation(g[:, h, m, :], yn[:, h, m, :], ACT.Gelu, bias=lnb[:, j, m:m + 1],
                                   scale=lng[:, j, m:m + 1]).then_inc(g_ready[h], 1)

            def k_exp(i, t):
                act.wait_ge(kv_ready, nth(i, NT, t))
                act.activation(E[:, t % HT, :], KV[:, t % HT, 0:D], ACT.Exp, bias=neg1[:, 0:1]).then_inc(e_ready, 1)

            def k_square(i, t):
                act.wait_ge(k_ready, nth(i, NT, t))
                act.activation(KS[:, t % HT, :], K[:, t % HT, :], ACT.Square).then_inc(ks_ready, 1)

            def k_root(i, h):
                act.wait_ge(sse_ready, nth(i, 2, h))
                act.activation(lnk[:], sse[:], ACT.Ln).then_inc(lnk_ready, 1)
                act.wait_ge(lnk_ready, nth(i, 2, h))
                act.activation(r0[:], lnk[:], ACT.Exp, scale=-0.5).then_inc(r0_ready, 1)

            def q_exp(i, h, m, first, last):
                r, n = rotating(i, ("q", h, m), last)
                act.wait_ge(rot_full[r], n + 1)
                if h:
                    act.wait_ge(q_ready, nth(i, 2 * NC, m))
                act.activation(eq[:, m, :], RB[r][:], ACT.Exp, bias=bqc[:, m:m + 1]).then_inc(eq_ready, 1)

            def m_copy(i):
                act.wait_ge(m_full, nth(i, 1, 0))
                act.activation(M[:].rearrange("p c d -> p (c d)"), AB[:], ACT.Copy).then_inc(m_ready, 1)

            for l in range(1, NL, 2):
                act.wait_ge(wT_full, l + 1)
                act.activation(WT[:, l].rearrange("p c d -> p (c d)"), bank[5 + l % 2][:], ACT.Copy
                               ).then_inc(wT_copied, 1)
            for h in range(2):
                for c in range(NC):
                    xt_copy(0, h, c, False, ahead=True)
            act.wait_ge(w_col, 64)
            act.wait_ge(vecs_ready, NBLK + 2)
            act.wait_ge(consts, 6)

            def body(i, first, last):
                squares(i, 0, 0)
                k_exp(i, 0)
                squares(i, 1, 0)
                k_exp(i, 1)
                k_square(i, 0)
                k_square(i, 1)
                rb_copy(i, 0, 0, last)
                k_exp(i, 2)
                k_exp(i, 3)
                k_square(i, 2)
                k_square(i, 3)
                k_root(i, 0)
                gelus(i, 0, 0)
                rb_copy(i, 1, 0, last)
                gelus(i, 1, 0)
                squares(i, 0, 1)
                k_exp(i, 4)
                squares(i, 1, 1)
                k_exp(i, 5)
                k_square(i, 4)
                k_exp(i, 6)
                k_square(i, 5)
                rb_copy(i, 0, 1, last)
                k_exp(i, 7)
                k_square(i, 6)
                k_square(i, 7)
                for m in range(NC):
                    q_exp(i, 0, m, first, last)
                k_root(i, 1)
                gelus(i, 0, 1)
                rb_copy(i, 1, 1, last)
                gelus(i, 1, 1)
                squares(i, 0, 2)
                for m in range(NC):
                    q_exp(i, 1, m, first, last)
                squares(i, 1, 2)
                m_copy(i)
                rb_copy(i, 0, 2, last)
                gelus(i, 0, 2)
                rb_copy(i, 1, 2, last)
                gelus(i, 1, 2)
                if not last:
                    for h in range(2):
                        for c in range(NC):
                            xt_copy(i + 1, h, c, last)

            batches(act, body)

        @block.vector
        def _(dve):
            steps = [0]

            def chained(ins):
                ins.then_inc(dve_prep, 1)
                steps[0] += 1
                dve.wait_ge(dve_prep, steps[0])

            def ln1_statistics(b, t):
                if t % HT == 0:
                    dve.wait_ge(x_loaded[t // HT], 16 * b + 16)
                dve.bn_stats(st1[:, t, :], X[:, t, :]).then_inc(ln1_stats, 1)

            def ln1_mean_var(b, h):
                dve.wait_ge(ln1_stats, nth(b, NT, h * HT + HT - 1))
                dve.sem_inc(stats_seen)
                for t in range(h * HT, (h + 1) * HT):
                    dve.bn_aggr(mv1[:, t, :], st1[:, t, :]).then_inc(ln1_mean, 1)
                dve.wait_ge(ln1_mean, nth(b, NT, h * HT + HT - 1))
                dve.tensor_scalar(ve1[:, h * HT:(h + 1) * HT], mv1[:, h * HT:(h + 1) * HT, 1], EPS_LN, None, ALU.add
                                  ).then_inc(ln1_var, 1)

            def ln1_normalise(b, h, ahead=False):
                dve.wait_ge(ln1_rstd, nth(b, 2, h))
                if not ahead:
                    dve.wait_ge(xn_based, nth(b - 1, 2, h))
                    dve.wait_ge(xT_ready, nth(b - 1, 2 * NC, h * NC + NC - 1))
                for t in range(h * HT, (h + 1) * HT):
                    dve.tensor_scalar(XN[:, t, :], X[:, t, :], mv1[:, t, 0:1], rs1[:, t:t + 1],
                                      ALU.subtract, ALU.mult).then_inc(xn_ready, 1)

            def ffn_var(i, h, j, last):
                r, n = rotating(i, ("var", h, j), last)
                dve.wait_ge(rot_full[r], n + 1)
                dve.tensor_scalar(vef[:, h, :], RB[r][:].rearrange("p (t n) -> p t n", t=HT)[:, :, 0], EPS_LN, None,
                                  ALU.add).then_inc(fvar_ready[h], 1)

            def ffn_normalise(i, h, j):
                dve.wait_ge(rb_ready[h], nth(i, NBLK, j))
                for m in range(NC):
                    dve.scalar_tensor_tensor(yn[:, h, m, :], FB[h][m][:], b1c[:, j, m:m + 1], rb[:, h, :],
                                             ALU.add, ALU.mult).then_inc(yn_ready[h], 1)

            def ffn_residual(i, h, j):
                for m in range(NC):
                    dve.wait_ge(ffn_full[h][m], nth(i, 2 * NBLK, 2 * j + 1))
                    before = xT[m] if j == 0 else hT[m]
                    dve.scalar_tensor_tensor(hT[m][:, half(h)], FB[h][m][:], fb[:, 2 * j + 1, m:m + 1],
                                             before[:, half(h)], ALU.add, ALU.add).then_inc(h_ready[h], 1)

            def kv_bias(i, t, first, last):
                r, n = rotating(i, ("kv", t), last)
                dve.wait_ge(rot_full[r], n + 1)
                if t >= HT:
                    dve.wait_ge(kvt_done, nth(i, NT, t - HT))
                elif not first:
                    dve.wait_ge(kvt_done, nth(i - 1, NT, t + HT))
                dve.tensor_tensor(KV[:, t % HT, :], RB[r][:], kvb[:], ALU.add).then_inc(kv_ready, 1)

            def k_elu(i, t):
                dve.wait_ge(e_ready, nth(i, NT, t))
                dve.scalar_tensor_tensor(K[:, t % HT, :], E[:, t % HT, :], 1.0, KV[:, t % HT, 0:D],
                                         ALU.min, ALU.max).then_inc(k_ready, 1)

            def k_sum(i, t):
                dve.wait_ge(ks_ready, nth(i, NT, t))
                dve.tensor_reduce(ss[:, t % HT, :], KS[:, t % HT, :].rearrange("p (h d) -> p h d", d=DEPTH),
                                  AX_X, ALU.add).then_inc(ss_ready, 1)

            def k_sum_eps(i, h):
                dve.wait_ge(ss_ready, nth(i, NT, h * HT + HT - 1))
                dve.tensor_scalar(sse[:], ss[:].rearrange("p t h -> p (t h)"), EPS_ATTN, None, ALU.add
                                  ).then_inc(sse_ready, 1)

            def k_newton(i, h):
                dve.wait_ge(r0_ready, nth(i, 2, h))
                dve.tensor_tensor(ra[:], r0[:], r0[:], ALU.mult).then_inc(ra_ready, 1)
                dve.wait_ge(ra_ready, nth(i, 2, h))
                dve.scalar_tensor_tensor(rc[:], ra[:], -0.5, sse[:], ALU.mult, ALU.mult).then_inc(rc_ready, 1)
                dve.wait_ge(rc_ready, nth(i, 2, h))
                dve.scalar_tensor_tensor(rk[:].rearrange("p t h -> p (t h)"), rc[:], 1.5, r0[:], ALU.add, ALU.mult
                                         ).then_inc(rk_ready, 1)

            def k_hat(i, t):
                dve.wait_ge(rk_ready, nth(i, 2, t // HT))
                dve.tensor_tensor(KH[:, t % HT, :].rearrange("p (h d) -> p h d", d=DEPTH),
                                  K[:, t % HT, :].rearrange("p (h d) -> p h d", d=DEPTH),
                                  rk[:, t % HT, :].unsqueeze(2).broadcast_to([P, NH, DEPTH]), ALU.mult
                                  ).then_inc(kh_ready, 1)

            def q_elu(i, h, last):
                for m in range(NC):
                    dve.wait_ge(eq_ready, nth(i, 2 * NC, h * NC + m))
                    dve.tensor_scalar(eq[:, m, :], eq[:, m, :], 1.0, None, ALU.min).then_inc(eq_min, 1)
                for m in range(NC):
                    r, n = rotating(i, ("q", h, m), last)
                    dve.wait_ge(eq_min, nth(i, 2 * NC, h * NC + m))
                    dve.scalar_tensor_tensor(qT[m][:, half(h)], RB[r][:], bq1[:, m:m + 1], eq[:, m, :],
                                             ALU.add, ALU.max).then_inc(q_ready, 1)

            def block_diagonal(i):
                dve.wait_ge(kvt_done, nth(i, NT, NT - 1))
                dve.tensor_tensor(BD[:].rearrange("p (c n) -> p c n", c=NC),
                                  AB[:, 0:NC * P].rearrange("p (c n) -> p c n", c=NC),
                                  head_mask[:].unsqueeze(1).broadcast_to([P, NC, P]), ALU.mult).then_inc(bd_ready, 1)

            def att_y(i, p, last):
                r, n = rotating(i, ("out", p), last)
                dve.wait_ge(rot_full[r], n + 1)
                dve.wait_ge(xn_based, nth(i, 2, p // 2))
                dve.tensor_tensor(Y[:, p % 2].rearrange("p t d -> p (t d)"), RB[r][:],
                                  XNB[:, 2 * p:2 * p + 2, :].rearrange("p t d -> p (t d)"), ALU.add
                                  ).then_inc(y_ready, 1)
                dve.wait_ge(y_ready, nth(i, NT // 2, p))
                for t in range(2):
                    dve.bn_stats(st2[:, 2 * p + t, :], Y[:, p % 2, t, :]).then_inc(ln2_stats, 1)
                dve.wait_ge(ln2_stats, nth(i, NT, 2 * p + 1))
                dve.sem_inc(stats_seen)
                for t in range(2):
                    dve.bn_aggr(mv2[:, 2 * p + t, :], st2[:, 2 * p + t, :]).then_inc(ln2_mean, 1)
                dve.wait_ge(ln2_mean, nth(i, NT, 2 * p + 1))
                dve.tensor_scalar(ve2[:, 2 * p:2 * p + 2], mv2[:, 2 * p:2 * p + 2, 1], EPS_ATTN, None, ALU.add
                                  ).then_inc(ln2_var, 1)

            def att_result(i, p):
                dve.wait_ge(x_based, nth(i, 2, p // 2))
                if p >= 2:
                    dve.wait_ge(res_ready, nth(i, NT, 2 * p - 3))
                for t in range(2):
                    dve.scalar_tensor_tensor(Z[:, 2 * (p % 2) + t, :], Y[:, p % 2, t, :], mv2[:, 2 * p + t, 0:1], gamma_r[:],
                                             ALU.subtract, ALU.mult).then_inc(z_ready, 1)
                dve.wait_ge(ln2_rstd, nth(i, NT // 2, p))
                for t in range(2):
                    n = 2 * p + t
                    dve.wait_ge(z_ready, nth(i, NT, n))
                    dve.scalar_tensor_tensor(RES[:, n, :], Z[:, 2 * (p % 2) + t, :], rs2[:, n:n + 1], RES[:, n, :],
                                             ALU.mult, ALU.add).then_inc(res_ready, 1)

            def finish(i, p, first, last):
                r, n = rotating(i, ("fin", p), last)
                dve.wait_ge(rot_full[r], n + 1)
                dve.wait_ge(res_ready, nth(i, NT, 2 * p + 1))
                if not first:
                    dve.wait_ge(stored[p // 2], 16 * i)
                dve.tensor_tensor(O[:, 2 * p:2 * p + 2, :].rearrange("p t d -> p (t d)"), RB[r][:],
                                  RES[:, 2 * p:2 * p + 2, :].rearrange("p t d -> p (t d)"), ALU.add
                                  ).then_inc(o_ready, 1)

            for h in range(2):
                for t in range(h * HT, (h + 1) * HT):
                    ln1_statistics(0, t)
                ln1_mean_var(0, h)
            for h in range(2):
                ln1_normalise(0, h, ahead=True)

            dve.wait_ge(w_row, 96)
            dve.wait_ge(w_col, 64)
            dve.tensor_scalar(bq1[:], bqc[:], 1.0, None, ALU.add).then_inc(vecs_ready, 1)
            chained(dve.tensor_reduce(b1m[:], b1_r[:], AX_X, ALU.add))
            chained(dve.tensor_scalar(b1m[:], b1m[:], -1.0 / D, None, ALU.mult))
            for j in range(NBLK):
                dve.tensor_scalar(b1c[:, j, :], fb[:, 2 * j, :], b1m[:, j:j + 1], None, ALU.add
                                  ).then_inc(vecs_ready, 1)
            dve.tensor_scalar(kvb[:, 0:D], kvb[:, 0:D], 1.0, None, ALU.add).then_inc(vecs_ready, 1)

            dve.wait_ge(w_q, 16)
            dve.wait_ge(w_sc, 16)
            dve.wait_ge(lbT_full, 1)
            for n in range(3):
                dve.tensor_copy(lbT[:, n * BANK:(n + 1) * BANK], bank[n][0:R, :]).then_inc(lbT_ready, 1)

            def dequantise(l):
                w = w_od[:, l % 2, :]
                if l >= 2:
                    dve.wait_ge(wT_full, l - 1)
                chained(dve.tensor_scalar(w, q_int[:, l].rearrange("p c d -> p (c d)"), 1.0 / 7.5, -1.0,
                                          ALU.mult, ALU.add))
                chained(dve.tensor_tensor(w.rearrange("p (g e) -> p g e", e=GROUP),
                                          w.rearrange("p (g e) -> p g e", e=GROUP),
                                          sc[:, l].rearrange("p c g -> p (c g)").unsqueeze(2)
                                          .broadcast_to([P, NC * NG, GROUP]), ALU.mult))
                dve.wait_ge(lora_full, l + 1)
                dve.tensor_tensor(w, w, bank[3 + l % 2][:], ALU.add).then_inc(w_od_ready, 1)

            def centre(l):
                b = bank[5 + l % 2]
                dve.wait_ge(wT_full, l + 1)
                chained(dve.tensor_reduce(wmean[:, 0, :], b[:].rearrange("p (c d) -> p c d", c=NC), AX_X, ALU.add))
                chained(dve.tensor_scalar(wmean[:, 1, :], wmean[:, 0, :], -1.0 / D, None, ALU.mult))
                for c in range(NC):
                    ins = dve.tensor_scalar(WT[:, l, c, :], b[:, c * D:(c + 1) * D], wmean[:, 1, c:c + 1], None,
                                            ALU.add)
                    ins.then_inc(wT_centred, 1)

            dve.wait_ge(vecs_ready, NBLK + 2)
            dve.wait_ge(consts, 6)
            for l in range(NL):
                dequantise(l)
                if l % 2 == 0:
                    centre(l)

            def body(i, first, last):
                kv_bias(i, 0, first, last)
                ffn_var(i, 0, 0, last)
                kv_bias(i, 1, first, last)
                k_elu(i, 0)
                k_elu(i, 1)
                ffn_var(i, 1, 0, last)
                k_sum(i, 0)
                ffn_normalise(i, 0, 0)
                kv_bias(i, 2, first, last)
                kv_bias(i, 3, first, last)
                k_elu(i, 2)
                k_elu(i, 3)
                k_sum(i, 1)
                k_sum(i, 2)
                k_sum(i, 3)
                k_sum_eps(i, 0)
                ffn_normalise(i, 1, 0)
                k_newton(i, 0)
                for t in range(HT):
                    k_hat(i, t)
                ffn_residual(i, 0, 0)
                ffn_residual(i, 1, 0)
                kv_bias(i, 4, first, last)
                ffn_var(i, 0, 1, last)
                kv_bias(i, 5, first, last)
                k_elu(i, 4)
                kv_bias(i, 6, first, last)
                k_elu(i, 5)
                ffn_var(i, 1, 1, last)
                k_sum(i, 4)
                ffn_normalise(i, 0, 1)
                kv_bias(i, 7, first, last)
                k_elu(i, 6)
                k_elu(i, 7)
                k_sum(i, 5)
                k_sum(i, 6)
                k_sum(i, 7)
                k_sum_eps(i, 1)
                q_elu(i, 0, last)
                ffn_normalise(i, 1, 1)
                k_newton(i, 1)
                for t in range(HT, NT):
                    k_hat(i, t)
                ffn_residual(i, 0, 1)
                ffn_residual(i, 1, 1)
                q_elu(i, 1, last)
                block_diagonal(i)
                ffn_var(i, 0, 2, last)
                att_y(i, 0, last)
                ffn_normalise(i, 0, 2)
                ffn_var(i, 1, 2, last)
                att_result(i, 0)
                att_y(i, 1, last)
                ffn_normalise(i, 1, 2)
                att_result(i, 1)
                if not last:
                    for t in range(NT):
                        ln1_statistics(i + 1, t)
                    ln1_mean_var(i + 1, 0)
                    ln1_mean_var(i + 1, 1)
                att_y(i, 2, last)
                att_y(i, 3, last)
                att_result(i, 2)
                att_result(i, 3)
                if not last:
                    ln1_normalise(i + 1, 0)
                    ln1_normalise(i + 1, 1)
                ffn_residual(i, 0, 2)
                ffn_residual(i, 1, 2)
                for p in range(NT // 2):
                    finish(i, p, first, last)

            batches(dve, body)

        @block.tensor
        def _(pe):
            def read_by(i, use):
                kind, *at = use
                return {
                    "var": lambda h, j: (fvar_ready[h], nth(i, NBLK, j)),
                    "rs": lambda h, j: (rb_ready[h], nth(i, NBLK, j)),
                    "kv": lambda t: (kv_ready, nth(i, NT, t)),
                    "q": lambda h, m: (q_ready, nth(i, 2 * NC, h * NC + m)),
                    "out": lambda p: (y_ready, nth(i, NT // 2, p)),
                    "xt": lambda h, c: (xT_ready, nth(i + 1, 2 * NC, h * NC + c)),
                    "fin": lambda p: (o_ready, nth(i, NT // 2, p)),
                }[kind](*at)

            def take(i, use, first, last):
                now = bank_uses(last)
                n = now.index(use)
                if n >= NROT:
                    before = read_by(i, now[n - NROT])
                elif first:
                    before = (xT_ready, AHEAD + n - NROT + 1)
                else:
                    before = read_by(i - 1, bank_uses(False)[n - NROT])
                pe.wait_ge(*before)
                return rotating(i, use, last)[0]

            def xt(b, h, c, last, ahead=False):
                if not ahead:
                    r = take(b - 1, ("xt", h, c), False, last)
                else:
                    r = (h * NC + c) % NROT
                    if h * NC + c >= NROT:
                        pe.wait_ge(xT_ready, h * NC + c - NROT + 1)
                pe.wait_ge(xn_ready, nth(b, NT, h * HT + HT - 1))
                for t in range(HT):
                    ins = pe.transpose(RB[r][:, t * P:(t + 1) * P], XN[:, h * HT + t, c * P:(c + 1) * P], ident[:])
                ins.then_inc(rot_full[r], 1)

            def first_linear(i, h, j):
                if j == 0:
                    pe.wait_ge(xT_ready, nth(i, 2 * NC, h * NC + NC - 1))
                else:
                    pe.wait_ge(h_ready[h], nth(i, NBLK * NC, j * NC - 1))
                src = xT if j == 0 else hT
                for m in range(NC):
                    for k in range(NC):
                        ins = pe.matmul(FB[h][m][:], WT[:, 2 * j, k, m * P:(m + 1) * P], src[k][:, half(h)],
                                        start=(k == 0), stop=(k == NC - 1))
                    ins.then_inc(ffn_full[h][m], 1)

            def second_linear(i, h, j):
                for m in range(NC):
                    pe.wait_ge(g_ready[h], nth(i, NBLK * NC, j * NC + NC - 1))
                    for k in range(NC):
                        ins = pe.matmul(FB[h][m][:], WT[:, 2 * j + 1, k, m * P:(m + 1) * P], g[:, h, k, :],
                                        start=(k == 0), stop=(k == NC - 1))
                    ins.then_inc(ffn_full[h][m], 1)

            def variance(i, h, j, first, last):
                r = take(i, ("var", h, j), first, last)
                pe.wait_ge(sqs_ready[h], nth(i, NBLK, j))
                for t in range(HT):
                    ins = pe.matmul(RB[r][:, t * P:(t + 1) * P], sqs[:, h, t * P:(t + 1) * P], mean_w[:],
                                    start=True, stop=True)
                ins.then_inc(rot_full[r], 1)

            def spread_rstd(i, h, j, first, last):
                r = take(i, ("rs", h, j), first, last)
                pe.wait_ge(frstd_ready[h], nth(i, NBLK, j))
                for t in range(HT):
                    ins = pe.transpose(RB[r][:, t * P:(t + 1) * P], rsf[:, h, t:t + 1].broadcast_to([P, P]), ident[:])
                ins.then_inc(rot_full[r], 1)

            def project_kv(i, t, first, last):
                r = take(i, ("kv", t), first, last)
                for k in range(NC):
                    ins = pe.matmul(RB[r][:], xT[k][:, t * P:(t + 1) * P], Wkv[:, k, :],
                                    start=(k == 0), stop=(k == NC - 1))
                ins.then_inc(rot_full[r], 1)

            def add_vk(i, t, first):
                pe.wait_ge(kh_ready, nth(i, NT, t))
                if t == 0 and not first:
                    pe.wait_ge(m_ready, nth(i - 1, 1, 0))
                for c in range(NC):
                    ins = pe.matmul(AB[:, c * P:(c + 1) * P], KV[:, t % HT, D + c * P:D + (c + 1) * P],
                                    KH[:, t % HT, c * P:(c + 1) * P], start=(t == 0 and c == 0),
                                    stop=(t == NT - 1), skip_group_check=True)
                ins.then_inc(kvt_done, 1)

            def project_q(i, h, first, last):
                for m in range(NC):
                    r = take(i, ("q", h, m), first, last)
                    for k in range(NC):
                        ins = pe.matmul(RB[r][:], Wqs[:, k, m * P:(m + 1) * P], xT[k][:, half(h)],
                                        start=(k == 0), stop=(k == NC - 1))
                    ins.then_inc(rot_full[r], 1)

            def make_m(i):
                pe.wait_ge(bd_ready, nth(i, 1, 0))
                for c in range(NC):
                    ins = pe.matmul(AB[:, c * D:(c + 1) * D], BD[:, c * P:(c + 1) * P], Wos[:, c, :],
                                    start=True, stop=True)
                ins.then_inc(m_full, 1)

            def attend(i, p, first, last):
                r = take(i, ("out", p), first, last)
                pe.wait_ge(q_ready, nth(i, 2 * NC, p // 2 * NC + NC - 1))
                pe.wait_ge(m_ready, nth(i, 1, 0))
                for t in range(2):
                    for c in range(NC):
                        ins = pe.matmul(RB[r][:, t * D:(t + 1) * D], qT[c][:, (2 * p + t) * P:(2 * p + t + 1) * P],
                                        M[:, c, :], start=(c == 0), stop=(c == NC - 1))
                ins.then_inc(rot_full[r], 1)

            def to_rows(i, p, first, last):
                r = take(i, ("fin", p), first, last)
                pe.wait_ge(h_ready[p // 2], nth(i, NBLK * NC, NBLK * NC - 1))
                for t in range(2):
                    for c in range(NC):
                        ins = pe.transpose(RB[r][:, t * D + c * P:t * D + (c + 1) * P],
                                           hT[c][:, (2 * p + t) * P:(2 * p + t + 1) * P], ident[:])
                ins.then_inc(rot_full[r], 1)

            pe.wait_ge(consts, 6)
            pe.wait_ge(w_lb, 16)
            for n in range(NL * NC):
                ins = pe.transpose(bank[n // 4][0:R, n % 4 * P:(n % 4 + 1) * P], lb[:, n // NC, n % NC, :], ident[:])
            ins.then_inc(lbT_full, 1)
            pe.wait_ge(w_la, 16)
            pe.wait_ge(lbT_ready, 3)
            for l in range(NL + 1):
                if l < NL:
                    if l >= 2:
                        pe.wait_ge(w_od_ready, l - 1)
                    for c in range(NC):
                        n = l * NC + c
                        ins = pe.matmul(bank[3 + l % 2][:, c * D:(c + 1) * D], lbT[:, n * P:(n + 1) * P], la[:, l, :],
                                        start=True, stop=True)
                    ins.then_inc(lora_full, 1)
                if l >= 1:
                    m = l - 1
                    pe.wait_ge(w_od_ready, m + 1)
                    if m >= 2:
                        if m % 2 == 0:
                            pe.wait_ge(wT_centred, NC * (m // 2))
                        else:
                            pe.wait_ge(wT_copied, m // 2)
                    for k in range(NC):
                        for c in range(NC):
                            ins = pe.transpose(bank[5 + m % 2][:, k * D + c * P:k * D + (c + 1) * P],
                                               w_od[:, m % 2, c * D + k * P:c * D + (k + 1) * P], ident[:])
                    ins.then_inc(wT_full, 1)
            pe.wait_ge(wT_centred, NC * NBLK)
            pe.wait_ge(wT_copied, NBLK)
            for h in range(2):
                for c in range(NC):
                    xt(0, h, c, False, ahead=True)
            pe.wait_ge(w_qkvo, 64)

            def body(i, first, last):
                first_linear(i, 0, 0)
                first_linear(i, 1, 0)
                variance(i, 0, 0, first, last)
                project_kv(i, 0, first, last)
                project_kv(i, 1, first, last)
                spread_rstd(i, 0, 0, first, last)
                variance(i, 1, 0, first, last)
                project_kv(i, 2, first, last)
                project_kv(i, 3, first, last)
                spread_rstd(i, 1, 0, first, last)
                second_linear(i, 0, 0)
                second_linear(i, 1, 0)
                for t in range(HT):
                    add_vk(i, t, first)
                first_linear(i, 0, 1)
                project_kv(i, 4, first, last)
                first_linear(i, 1, 1)
                variance(i, 0, 1, first, last)
                project_kv(i, 5, first, last)
                project_kv(i, 6, first, last)
                spread_rstd(i, 0, 1, first, last)
                variance(i, 1, 1, first, last)
                project_kv(i, 7, first, last)
                project_q(i, 0, first, last)
                spread_rstd(i, 1, 1, first, last)
                second_linear(i, 0, 1)
                second_linear(i, 1, 1)
                for t in range(HT, NT):
                    add_vk(i, t, first)
                first_linear(i, 0, 2)
                project_q(i, 1, first, last)
                first_linear(i, 1, 2)
                variance(i, 0, 2, first, last)
                make_m(i)
                spread_rstd(i, 0, 2, first, last)
                attend(i, 0, first, last)
                variance(i, 1, 2, first, last)
                attend(i, 1, first, last)
                spread_rstd(i, 1, 2, first, last)
                attend(i, 2, first, last)
                second_linear(i, 0, 2)
                attend(i, 3, first, last)
                second_linear(i, 1, 2)
                if not last:
                    for h in range(2):
                        for c in range(NC):
                            xt(i + 1, h, c, last)
                for p in range(NT // 2):
                    to_rows(i, p, first, last)

            batches(pe, body)


_INS = ["L0_attn_x", "L0_attn_Wq", "L0_attn_bq", "L0_attn_Wk", "L0_attn_bk", "L0_attn_Wv", "L0_attn_bv",
        "L0_attn_Wo", "L0_attn_bo", "L0_attn_gamma", "L0_attn_beta", "L0_ffn_qweights", "L0_ffn_scales",
        "L0_ffn_biases", "L0_ffn_lora_a", "L0_ffn_lora_b", "L0_ffn_ln_gamma", "L0_ffn_ln_beta"]
_OUTS = [((8, 1024, 256), "float32")]


def kernel(**inputs):
    import numpy as _np
    import concourse.bacc as _bacc
    from concourse import mybir as _mybir
    from concourse.bass_utils import run_bass_kernel_spmd as _run

    nc = _bacc.Bacc("TRN2", target_bir_lowering=False, num_devices=1)
    arrays, args = {}, []
    for name in _INS:
        a = _np.ascontiguousarray(inputs[name])
        arrays[f"in_{name}_dram"] = a
        args.append(nc.dram_tensor(f"in_{name}_dram", a.shape, _mybir.dt.from_np(a.dtype), kind="ExternalInput").ap())
    for i, (shape, dtype) in enumerate(_OUTS):
        dt = _mybir.dt.from_np(_np.dtype(dtype))
        args.append(nc.dram_tensor(f"out_{i}_dram", shape, dt, kind="ExternalOutput").ap())
    block_kernel(nc, *args)
    r = _run(nc, [arrays], core_ids=[0])
    got = tuple(r.results[0][f"out_{i}_dram"] for i in range(len(_OUTS)))
    return got[0]
```

```python
from contextlib import ExitStack

import concourse.bass as bass
from concourse import mybir

ALU = mybir.AluOpType
ACT = mybir.ActivationFunctionType
F32 = mybir.dt.float32
I32 = mybir.dt.int32
F32R = mybir.dt.float32r
AX_X = mybir.AxisListType.X

P = 128
BANK = 512
NT = 8
HT = NT // 2
NBLK = 3
DEPTH = 16
GROUP = 16
EPS_LN = 1e-5
EPS_ATTN = 1e-6

def bank_uses(last):
    uses = [
        ("kv", 0), ("var", 0, 0), ("kv", 1), ("rs", 0, 0), ("kv", 2), ("var", 1, 0), ("kv", 3), ("rs", 1, 0),
        ("kv", 4), ("kv", 5), ("var", 0, 1), ("rs", 0, 1), ("kv", 6), ("var", 1, 1), ("kv", 7), ("rs", 1, 1),
        ("q", 0, 0), ("q", 0, 1), ("q", 1, 0), ("q", 1, 1), ("var", 0, 2), ("xt", 0, 0), ("rs", 0, 2),
        ("var", 1, 2), ("out", 0), ("rs", 1, 2), ("xt", 0, 1), ("out", 1), ("xt", 1, 0), ("out", 2),
        ("fin", 0), ("xt", 1, 1), ("fin", 1), ("out", 3), ("fin", 2), ("fin", 3)
    ]
    return [use for use in uses if not (last and use[0] == "xt")]


USES = len(bank_uses(False))
NROT = 3
AHEAD = 4
assert USES % NROT == 0


def rotating(i, use, last):
    n = AHEAD + bank_uses(last).index(use)
    return n % NROT, i * (USES // NROT) + n // NROT


def nth(i, per, n):
    return i * per + (n + 1)


def block_kernel(nc: bass.Bass, x, Wq, bq, Wk, bk, Wv, bv, Wo, bo, gamma, beta,
                 qweights, scales, biases, lora_a, lora_b, ln_gamma, ln_beta, out):
    NB, S, D = x.shape
    NL = qweights.shape[0]
    R = lora_a.shape[1]
    NC = D // P
    NG = D // GROUP
    NH = D // DEPTH
    assert S == NT * P and NC == 2 and NL == 2 * NBLK and D == 256

    x_rows = x.rearrange("b (p t) d -> b p t d", t=NT)
    out_rows = out.rearrange("b (p t) d -> b p t d", t=NT)

    ctx = ExitStack()
    with ctx:
        def sb(name, shape, dt=F32):
            return ctx.enter_context(nc.sbuf_tensor(name, shape, dt))

        def sem(name):
            return ctx.enter_context(nc.semaphore(name))

        sc = sb("sc", [P, NL, NC, NG])
        lb = sb("lb", [P, NL, NC, R])
        WTh = sb("WTh", [P, NL, NC, D], F32R)
        WTl = sb("WTl", [P, NL, NC, D], F32R)
        Wqs = sb("Wqs", [P, NC, D])
        Wqh = sb("Wqh", [P, NC, D], F32R)
        Wql = sb("Wql", [P, NC, D], F32R)
        Wkv = sb("Wkv", [P, NC, 2 * D])
        Wkvh = sb("Wkvh", [P, NC, 2 * D], F32R)
        Wkvl = sb("Wkvl", [P, NC, 2 * D], F32R)
        Wos = sb("Wos", [P, NC, D])
        ident = sb("ident", [P, P])
        head_mask = sb("head_mask", [P, P])
        mean_w = sb("mean_w", [P, P])
        ln_dummy = sb("ln_dummy", [P, 1])
        neg1 = sb("neg1", [P, 1])
        neghalf = sb("neghalf", [P, HT])
        kvb = sb("kvb", [P, 2 * D])
        bo_r = sb("bo_r", [P, D])
        gamma_r = sb("gamma_r", [P, D])
        beta_r = sb("beta_r", [P, D])
        b1_r = sb("b1_r", [P, NBLK, D])
        fb = sb("fb", [P, NL, NC])
        lng = sb("lng", [P, NBLK, NC])
        lnb = sb("lnb", [P, NBLK, NC])
        bqc = sb("bqc", [P, NC])
        bq1 = sb("bq1", [P, NC])
        b1c = sb("b1c", [P, NBLK, NC])
        b1m = sb("b1m", [P, NBLK])
        wmean = sb("wmean", [P, 2, NC])
        X = sb("X", [P, NT, D])
        XN = sb("XN", [P, NT, D])
        XNB = sb("XNB", [P, NT, D])
        RES = sb("RES", [P, NT, D])
        xT = [sb(f"xT{c}", [P, S]) for c in range(NC)]
        hT = [sb(f"hT{c}", [P, S]) for c in range(NC)]
        xTh, xTl, hTh, hTl = ([sb(f"{n}{c}", [P, S], F32R) for c in range(NC)] for n in ("xTh", "xTl", "hTh", "hTl"))
        qT = [sb(f"qT{c}", [P, S]) for c in range(NC)]

        def lbT(n):
            return qT[n // NT][0:R, n % NT * P:(n % NT + 1) * P]

        st1 = sb("st1", [P, NT, 6])
        mv1 = sb("mv1", [P, NT, 2])
        ve1 = sb("ve1", [P, NT])
        rs1 = sb("rs1", [P, NT])
        st2 = sb("st2", [P, NT, 6])
        mv2 = sb("mv2", [P, NT, 2])
        ve2 = sb("ve2", [P, NT])
        rs2 = sb("rs2", [P, NT])
        fw = sb("fw", [P, 2, NC, BANK])
        sqs = sb("sqs", [P, 2, BANK])
        vef = sb("vef", [P, 2, HT])
        rsf = sb("rsf", [P, 2, HT])
        q_int = [fw[:, l // NC, l % NC, :].bitcast(I32) for l in range(4)]
        q_int += [hT[0][:].bitcast(I32)[:, l * NC * D:(l + 1) * NC * D] for l in range(2)]
        rb = sb("rb", [P, 2, BANK])
        gh = sb("gh", [P, 2, NC, BANK], F32R)
        gl = sb("gl", [P, 2, NC, BANK], F32R)
        KV = sb("KV", [P, HT, 2 * D])
        E = sb("E", [P, HT, D])
        K = sb("K", [P, HT, D])
        ss = sb("ss", [P, HT, NH])
        sse = sb("sse", [P, HT * NH])
        lnk = sb("lnk", [P, HT * NH])
        r0 = sb("r0", [P, HT * NH])
        ra = sb("ra", [P, HT * NH])
        rc = sb("rc", [P, HT * NH])
        rk = sb("rk", [P, HT, NH])
        eq = sb("eq", [P, NC, BANK])
        la = [hT[1][0:R, l * D:(l + 1) * D] for l in range(4)] + [eq[0:R, 0, l * D:(l + 1) * D] for l in range(2)]
        BD = sb("BD", [P, NC * P])
        M = sb("M", [P, NC, D])
        Y = sb("Y", [P, 2, 2, D])
        w_od = Y[:].rearrange("p s c d -> p s (c d)")
        WT = E[:].rearrange("p (s c) d -> p s c d", c=NC)

        bank = [ctx.enter_context(nc.psum_tensor(f"bank{n}", [P, BANK], F32)) for n in range(8)]
        FB = [bank[0:2], bank[2:4]]
        AB = bank[4]
        RB = bank[5:8]

        w_q, w_sc, w_la, w_lb, w_qkvo, w_row, w_col = (
            sem(n) for n in ("w_q", "w_sc", "w_la", "w_lb", "w_qkvo", "w_row", "w_col"))
        consts = sem("consts")
        consts_step = sem("consts_step")
        dve_prep = sem("dve_prep")
        lbT_full = sem("lbT_full")
        lbT_ready = sem("lbT_ready")
        lora_full = sem("lora_full")
        w_od_ready = sem("w_od_ready")
        wT_full = sem("wT_full")
        wT_centred = sem("wT_centred")
        wT_copied = sem("wT_copied")
        wT_high = sem("wT_high")
        wT_split = sem("wT_split")
        wkvq_high = sem("wkvq_high")
        wkvq_split = sem("wkvq_split")
        xT_high, xT_low = sem("xT_high"), sem("xT_low")
        g_high, h_high = ([sem(f"{n}{h}") for h in range(2)] for n in ("g_high", "h_high"))
        g_low, h_low = ([[sem(f"{n}{h}{m}") for m in range(NC)] for h in range(2)] for n in ("g_low", "h_low"))
        vecs_ready = sem("vecs_ready")
        x_loaded = [sem(f"x_loaded{h}") for h in range(2)]
        x_based = sem("x_based")
        xn_based = sem("xn_based")
        ln1_stats, ln1_mean, ln1_var, ln1_rstd, xn_ready = (
            sem(n) for n in ("ln1_stats", "ln1_mean", "ln1_var", "ln1_rstd", "xn_ready"))
        stats_seen = sem("stats_seen")
        xT_ready = sem("xT_ready")
        rot_full = [sem(f"rot_full{n}") for n in range(NROT)]
        ffn_full = [[sem(f"ffn_full{h}{m}") for m in range(NC)] for h in range(2)]
        m_full = sem("m_full")
        sq_ready, sqs_ready, fvar_ready, frstd_ready, rb_ready, yn_ready, g_ready, h_ready = (
            [sem(f"{n}{h}") for h in range(2)]
            for n in ("sq_ready", "sqs_ready", "fvar_ready", "frstd_ready", "rb_ready", "yn_ready", "g_ready",
                      "h_ready"))
        kv_ready, e_ready, k_ready, ks_ready, ss_ready, sse_ready, lnk_ready, r0_ready, ra_ready, rc_ready, rk_ready, \
            kh_ready, kvt_done = (sem(n) for n in (
                "kv_ready", "e_ready", "k_ready", "ks_ready", "ss_ready", "sse_ready", "lnk_ready", "r0_ready",
                "ra_ready", "rc_ready", "rk_ready", "kh_ready", "kvt_done"))
        eq_ready, eq_min, q_ready, bd_ready, m_ready = (
            sem(n) for n in ("eq_ready", "eq_min", "q_ready", "bd_ready", "m_ready"))
        y_ready, ln2_stats, ln2_mean, ln2_var, ln2_rstd, z_ready, res_ready = (
            sem(n) for n in ("y_ready", "ln2_stats", "ln2_mean", "ln2_var", "ln2_rstd", "z_ready", "res_ready"))
        o_ready = sem("o_ready")
        stored = [sem(f"stored{h}") for h in range(2)]

        def half(h):
            return slice(h * BANK, (h + 1) * BANK)

        def batches(engine, body):
            body(0, True, False)
            with engine.Fori(1, NB - 1) as i:
                body(i, False, False)
            body(NB - 1, False, True)

        block = ctx.enter_context(nc.Block())

        def g_lower(engine, i, h, j, m):
            engine.wait_ge(g_high[h], nth(i, NBLK * NC, j * NC + m))
            engine.tensor_tensor(gl[:, h, m, :], fw[:, h, m, :], gh[:, h, m, :].bitcast(F32), ALU.subtract
                                 ).then_inc(g_low[h][m], 1)

        def h_lower(engine, i, h, j, m):
            engine.wait_ge(h_high[h], nth(i, (NBLK - 1) * NC, j * NC + m))
            engine.tensor_tensor(hTl[m][:, half(h)], hT[m][:, half(h)], hTh[m][:, half(h)].bitcast(F32), ALU.subtract
                                 ).then_inc(h_low[h][m], 1)

        @block.sync
        def _(sp):
            def load_x(b, h):
                sp.dma_start(X[:, h * HT:(h + 1) * HT, :],
                             x_rows[bass.ds(b, 1), :, h * HT:(h + 1) * HT, :].rearrange("o p t d -> (o p) t d")
                             ).then_inc(x_loaded[h], 16)

            load_x(0, 0)
            load_x(0, 1)
            for c, (w, dst) in enumerate(((Wk, Wkv[:, :, 0:D]), (Wv, Wkv[:, :, D:]), (Wq, Wqs[:]), (Wo, Wos[:]))):
                sp.dma_start(dst, w.rearrange("(c p) n -> p c n", p=P)).then_inc(w_qkvo, 16)
            for l in range(NL):
                sp.dma_start(la[l], lora_a[l]).then_inc(w_la, 16)

            def body(i, first, last):
                for h in range(2):
                    if not last:
                        sp.wait_ge(x_based, nth(i, 2, h))
                        load_x(i + 1, h)
                for h in range(2):
                    sp.wait_ge(o_ready, nth(i, NT // 2, 2 * h + 1))
                    sp.dma_start(out_rows[bass.ds(i, 1), :, h * HT:(h + 1) * HT, :].rearrange("o p t d -> (o p) t d"),
                                 RES[:, h * HT:(h + 1) * HT, :]).then_inc(stored[h], 16)

            batches(sp, body)
            for h in range(2):
                sp.wait_ge(stored[h], 16 * NB)

        @block.gpsimd
        def _(pool):
            pool.memset(ident[:], 0.0).then_inc(consts_step, 1)
            pool.memset(head_mask[:], 1.0).then_inc(consts_step, 1)
            pool.memset(mean_w[:], 1.0 / D).then_inc(consts, 1)
            pool.memset(neg1[:], -1.0).then_inc(consts, 1)
            pool.memset(neghalf[:], -0.5).then_inc(consts, 1)
            pool.wait_ge(consts_step, 2)
            pool.affine_select(out=ident[:], in_=ident[:], compare_op=ALU.not_equal, fill=1.0,
                               base=0, pattern=[[-1, P]], channel_multiplier=1).then_inc(consts, 1)
            heads = head_mask[:].rearrange("p (h d) -> p h d", d=DEPTH)
            pool.affine_select(out=heads, in_=heads, compare_op=ALU.is_ge, fill=0.0, base=0,
                               pattern=[[-DEPTH, P // DEPTH], [0, DEPTH]], channel_multiplier=1
                               ).then_inc(consts_step, 1)
            pool.wait_ge(consts_step, 3)
            pool.affine_select(out=heads, in_=heads, compare_op=ALU.is_ge, fill=0.0, base=DEPTH - 1,
                               pattern=[[DEPTH, P // DEPTH], [0, DEPTH]], channel_multiplier=-1).then_inc(consts, 1)

            def rstd(dst, var, n):
                return pool.tensor_tensor(dst, var, neghalf[:, 0:n], ALU.pow)

            def ln1_root(b, h):
                pool.wait_ge(ln1_var, nth(b, 2, h))
                rstd(rs1[:, h * HT:(h + 1) * HT], ve1[:, h * HT:(h + 1) * HT], HT).then_inc(ln1_rstd, 1)

            def base_x(i, h, first):
                pool.wait_ge(xn_ready, nth(i, NT, h * HT + HT - 1))
                if not first:
                    pool.wait_ge(stored[h], 16 * i)
                pool.tensor_tensor(RES[:, h * HT:(h + 1) * HT, :], X[:, h * HT:(h + 1) * HT, :],
                                   beta_r[:].unsqueeze(1).broadcast_to([P, HT, D]), ALU.add).then_inc(x_based, 1)

            def base_xn(i, h, first):
                pool.wait_ge(xn_ready, nth(i, NT, h * HT + HT - 1))
                if not first:
                    pool.wait_ge(y_ready, nth(i - 1, NT // 2, 2 * h + 1))
                pool.tensor_tensor(XNB[:, h * HT:(h + 1) * HT, :], XN[:, h * HT:(h + 1) * HT, :],
                                   bo_r[:].unsqueeze(1).broadcast_to([P, HT, D]), ALU.add).then_inc(xn_based, 1)

            def add_squares(i, h, j):
                pool.wait_ge(sq_ready[h], nth(i, NBLK * NC, j * NC + NC - 1))
                pool.tensor_tensor(sqs[:, h, :], fw[:, h, 0, :], fw[:, h, 1, :], ALU.add).then_inc(sqs_ready[h], 1)

            def ffn_root(i, h, j):
                pool.wait_ge(fvar_ready[h], nth(i, NBLK, j))
                rstd(rsf[:, h, :], vef[:, h, :], HT).then_inc(frstd_ready[h], 1)

            def ln2_root(i, p):
                pool.wait_ge(ln2_var, nth(i, NT // 2, p))
                rstd(rs2[:, 2 * p:2 * p + 2], ve2[:, 2 * p:2 * p + 2], 2).then_inc(ln2_rstd, 1)

            for h in range(2):
                ln1_root(0, h)
            pool.wait_ge(w_row, 96)
            pool.wait_ge(consts, 5)

            def body(i, first, last):
                base_x(i, 0, first)
                add_squares(i, 0, 0)
                ffn_root(i, 0, 0)
                add_squares(i, 1, 0)
                ffn_root(i, 1, 0)
                base_x(i, 1, first)
                if not last:
                    ln1_root(i + 1, 0)
                g_lower(pool, i, 1, 0, 1)
                h_lower(pool, i, 0, 0, 0)
                h_lower(pool, i, 0, 0, 1)
                base_xn(i, 0, first)
                add_squares(i, 0, 1)
                ffn_root(i, 0, 1)
                add_squares(i, 1, 1)
                ffn_root(i, 1, 1)
                g_lower(pool, i, 0, 1, 1)
                base_xn(i, 1, first)
                if not last:
                    ln1_root(i + 1, 1)
                h_lower(pool, i, 0, 1, 0)
                h_lower(pool, i, 0, 1, 1)
                add_squares(i, 0, 2)
                ffn_root(i, 0, 2)
                add_squares(i, 1, 2)
                ffn_root(i, 1, 2)
                ln2_root(i, 0)
                g_lower(pool, i, 0, 2, 0)
                g_lower(pool, i, 0, 2, 1)
                ln2_root(i, 1)
                g_lower(pool, i, 1, 2, 0)
                g_lower(pool, i, 1, 2, 1)
                ln2_root(i, 2)
                ln2_root(i, 3)

            batches(pool, body)

        @block.scalar
        def _(act):
            for l in range(NL):
                act.dma_start(q_int[l].rearrange("p (c d) -> p c d", c=NC), qweights[l].rearrange("(c p) d -> p c d", p=P)
                              ).then_inc(w_q, 16)
            act.dma_start(sc[:], scales.rearrange("l (c p) g -> p l c g", p=P)).then_inc(w_sc, 16)
            act.dma_start(lb[:], lora_b.rearrange("l (c p) r -> p l c r", p=P)).then_inc(w_lb, 16)
            for dst, src in ((kvb[:, 0:D], bk), (kvb[:, D:], bv), (bo_r[:], bo), (gamma_r[:], gamma), (beta_r[:], beta)):
                act.dma_start(dst, src.unsqueeze(0).broadcast_to([P, D])).then_inc(w_row, 16)
            act.dma_start(b1_r[:], biases.rearrange("(j two) d -> two j d", two=2)[0:1]
                          .broadcast_to([P, NBLK, D])).then_inc(w_row, 16)
            with nc.allow_non_contiguous_dma(reason="short vectors, feature on the partition"):
                act.dma_start(fb[:], biases.rearrange("l (c p) -> p l c", p=P)).then_inc(w_col, 16)
                act.dma_start(lng[:], ln_gamma.rearrange("l (c p) -> p l c", p=P)).then_inc(w_col, 16)
                act.dma_start(lnb[:], ln_beta.rearrange("l (c p) -> p l c", p=P)).then_inc(w_col, 16)
                act.dma_start(bqc[:], bq.rearrange("(c p) -> p c", p=P)).then_inc(w_col, 16)

            def xt_copy(b, h, c, last, ahead=False):
                r, n = (h * NC + c) % NROT, (h * NC + c) // NROT
                if not ahead:
                    r, n = rotating(b - 1, ("xt", h, c), last)
                    act.wait_ge(h_ready[h], nth(b - 1, NBLK * NC, c))
                act.wait_ge(rot_full[r], n + 1)
                act.activation(xTh[c][:, half(h)], RB[r][:], ACT.Copy).then_inc(xT_high, 1)
                act.activation(xT[c][:, half(h)], RB[r][:], ACT.Copy).then_inc(xT_ready, 1)

            def square(i, h, j, m):
                act.wait_ge(ffn_full[h][m], nth(i, 2 * NBLK, 2 * j))
                act.activation(fw[:, h, m, :], FB[h][m][:], ACT.Square, bias=b1c[:, j, m:m + 1]
                               ).then_inc(sq_ready[h], 1)

            def rb_copy(i, h, j, last):
                r, n = rotating(i, ("rs", h, j), last)
                act.wait_ge(rot_full[r], n + 1)
                act.activation(rb[:, h, :], RB[r][:], ACT.Copy).then_inc(rb_ready[h], 1)

            def gelu(i, h, j, m):
                act.wait_ge(yn_ready[h], nth(i, NBLK * NC, j * NC + m))
                act.activation(fw[:, h, m, :], fw[:, h, m, :], ACT.Gelu, bias=lnb[:, j, m:m + 1],
                               scale=lng[:, j, m:m + 1]).then_inc(g_ready[h], 1)

            def g_higher(i, h, j, m):
                act.wait_ge(g_ready[h], nth(i, NBLK * NC, j * NC + m))
                act.activation(gh[:, h, m, :], fw[:, h, m, :], ACT.Copy).then_inc(g_high[h], 1)

            def h_higher(i, h, j, m):
                act.wait_ge(h_ready[h], nth(i, NBLK * NC, j * NC + m))
                act.activation(hTh[m][:, half(h)], hT[m][:, half(h)], ACT.Copy).then_inc(h_high[h], 1)

            def exp_ln_tables():
                act.activation(ln_dummy[:], mean_w[:, 0:1], ACT.Ln)

            def k_exp(i, t):
                act.wait_ge(kv_ready, nth(i, NT, t))
                act.activation(E[:, t % HT, :], KV[:, t % HT, 0:D], ACT.Exp, bias=neg1[:, 0:1]).then_inc(e_ready, 1)

            def k_square(i, t):
                act.wait_ge(k_ready, nth(i, NT, t))
                act.activation(E[:, t % HT, :], K[:, t % HT, :], ACT.Square).then_inc(ks_ready, 1)

            def k_root(i, h):
                act.wait_ge(sse_ready, nth(i, 2, h))
                act.activation(lnk[:], sse[:], ACT.Ln).then_inc(lnk_ready, 1)
                act.wait_ge(lnk_ready, nth(i, 2, h))
                act.activation(r0[:], lnk[:], ACT.Exp, scale=-0.5).then_inc(r0_ready, 1)

            def q_exp(i, h, m, last):
                r, n = rotating(i, ("q", h, m), last)
                act.wait_ge(rot_full[r], n + 1)
                if h:
                    act.wait_ge(q_ready, nth(i, 2 * NC, m))
                act.activation(eq[:, m, :], RB[r][:], ACT.Exp, bias=bqc[:, m:m + 1]).then_inc(eq_ready, 1)

            def m_copy(i):
                act.wait_ge(m_full, nth(i, 1, 0))
                act.activation(M[:].rearrange("p c d -> p (c d)"), AB[:], ACT.Copy).then_inc(m_ready, 1)

            for h in range(2):
                for c in range(NC):
                    xt_copy(0, h, c, False, ahead=True)
            act.wait_ge(w_qkvo, 64)
            act.activation(Wkvh[:], Wkv[:], ACT.Copy).then_inc(wkvq_high, 1)
            act.activation(Wqh[:], Wqs[:], ACT.Copy).then_inc(wkvq_high, 1)
            for l in range(NL):
                if l % 2:
                    act.wait_ge(wT_full, l + 1)
                    if l >= 2:
                        act.wait_ge(wT_split, l - 1)
                    act.activation(WT[:, 1].rearrange("p c d -> p (c d)"), bank[4][:], ACT.Copy
                                   ).then_inc(wT_copied, 1)
                    act.wait_ge(wT_copied, l // 2 + 1)
                else:
                    act.wait_ge(wT_centred, NC * (l // 2 + 1))
                act.activation(WTh[:, l], WT[:, l % 2], ACT.Copy).then_inc(wT_high, 1)
            act.wait_ge(w_col, 64)
            act.wait_ge(vecs_ready, NBLK + 2)
            act.wait_ge(consts, 5)

            def body(i, first, last):
                square(i, 0, 0, 0)
                square(i, 0, 0, 1)
                square(i, 1, 0, 0)
                square(i, 1, 0, 1)
                exp_ln_tables()
                k_exp(i, 0)
                rb_copy(i, 0, 0, last)
                k_exp(i, 1)
                gelu(i, 0, 0, 0)
                gelu(i, 0, 0, 1)
                rb_copy(i, 1, 0, last)
                g_higher(i, 0, 0, 0)
                g_higher(i, 0, 0, 1)
                gelu(i, 1, 0, 0)
                g_higher(i, 1, 0, 0)
                gelu(i, 1, 0, 1)
                g_higher(i, 1, 0, 1)
                h_higher(i, 0, 0, 0)
                k_square(i, 0)
                h_higher(i, 0, 0, 1)
                exp_ln_tables()
                k_exp(i, 2)
                k_exp(i, 3)
                k_square(i, 1)
                k_square(i, 2)
                h_higher(i, 1, 0, 0)
                square(i, 0, 1, 0)
                h_higher(i, 1, 0, 1)
                k_square(i, 3)
                square(i, 0, 1, 1)
                k_root(i, 0)
                square(i, 1, 1, 0)
                square(i, 1, 1, 1)
                k_exp(i, 4)
                rb_copy(i, 0, 1, last)
                k_exp(i, 5)
                gelu(i, 0, 1, 0)
                gelu(i, 0, 1, 1)
                rb_copy(i, 1, 1, last)
                g_higher(i, 0, 1, 0)
                g_higher(i, 0, 1, 1)
                gelu(i, 1, 1, 0)
                g_higher(i, 1, 1, 0)
                gelu(i, 1, 1, 1)
                g_higher(i, 1, 1, 1)
                k_square(i, 4)
                k_square(i, 5)
                exp_ln_tables()
                q_exp(i, 0, 0, last)
                h_higher(i, 0, 1, 0)
                k_exp(i, 6)
                k_exp(i, 7)
                h_higher(i, 0, 1, 1)
                k_square(i, 6)
                k_square(i, 7)
                h_higher(i, 1, 1, 0)
                q_exp(i, 0, 1, last)
                k_root(i, 1)
                h_higher(i, 1, 1, 1)
                square(i, 0, 2, 0)
                square(i, 0, 2, 1)
                q_exp(i, 1, 0, last)
                square(i, 1, 2, 0)
                q_exp(i, 1, 1, last)
                square(i, 1, 2, 1)
                if not last:
                    xt_copy(i + 1, 0, 0, last)
                rb_copy(i, 0, 2, last)
                m_copy(i)
                gelu(i, 0, 2, 0)
                rb_copy(i, 1, 2, last)
                if not last:
                    xt_copy(i + 1, 0, 1, last)
                gelu(i, 0, 2, 1)
                g_higher(i, 0, 2, 0)
                gelu(i, 1, 2, 0)
                g_higher(i, 0, 2, 1)
                g_higher(i, 1, 2, 0)
                gelu(i, 1, 2, 1)
                g_higher(i, 1, 2, 1)
                if not last:
                    xt_copy(i + 1, 1, 0, last)
                    xt_copy(i + 1, 1, 1, last)

            batches(act, body)

        @block.vector
        def _(dve):
            steps = [0]

            def chained(ins):
                ins.then_inc(dve_prep, 1)
                steps[0] += 1
                dve.wait_ge(dve_prep, steps[0])

            def ln1_statistics(b, h):
                dve.wait_ge(x_loaded[h], 16 * b + 16)
                for t in range(h * HT, (h + 1) * HT):
                    dve.bn_stats(st1[:, t, :], X[:, t, :]).then_inc(ln1_stats, 1)

            def ln1_mean_var(b, h):
                dve.wait_ge(ln1_stats, nth(b, NT, h * HT + HT - 1))
                dve.sem_inc(stats_seen)
                for t in range(h * HT, (h + 1) * HT):
                    dve.bn_aggr(mv1[:, t, :], st1[:, t, :]).then_inc(ln1_mean, 1)
                dve.wait_ge(ln1_mean, nth(b, NT, h * HT + HT - 1))
                dve.tensor_scalar(ve1[:, h * HT:(h + 1) * HT], mv1[:, h * HT:(h + 1) * HT, 1], EPS_LN, None, ALU.add
                                  ).then_inc(ln1_var, 1)

            def ln1_normalise(b, h, ahead=False):
                dve.wait_ge(ln1_rstd, nth(b, 2, h))
                if not ahead:
                    dve.wait_ge(xT_ready, nth(b - 1, 2 * NC, h * NC + NC - 1))
                    dve.wait_ge(xn_based, nth(b - 1, 2, h))
                for t in range(h * HT, (h + 1) * HT):
                    dve.tensor_scalar(XN[:, t, :], X[:, t, :], mv1[:, t, 0:1], rs1[:, t:t + 1],
                                      ALU.subtract, ALU.mult).then_inc(xn_ready, 1)

            def xt_low(b, h, c):
                dve.wait_ge(xT_ready, nth(b, 2 * NC, h * NC + c))
                dve.tensor_tensor(xTl[c][:, half(h)], xT[c][:, half(h)], xTh[c][:, half(h)].bitcast(F32),
                                  ALU.subtract).then_inc(xT_low, 1)

            def ffn_var(i, h, j, last):
                r, n = rotating(i, ("var", h, j), last)
                dve.wait_ge(rot_full[r], n + 1)
                dve.tensor_scalar(vef[:, h, :], RB[r][:].rearrange("p (t n) -> p t n", t=HT)[:, :, 0], EPS_LN, None,
                                  ALU.add).then_inc(fvar_ready[h], 1)

            def ffn_normalise(i, h, j, m):
                dve.wait_ge(rb_ready[h], nth(i, NBLK, j))
                dve.scalar_tensor_tensor(fw[:, h, m, :], FB[h][m][:], b1c[:, j, m:m + 1], rb[:, h, :],
                                         ALU.add, ALU.mult).then_inc(yn_ready[h], 1)

            def ffn_residual(i, h, j, m):
                dve.wait_ge(ffn_full[h][m], nth(i, 2 * NBLK, 2 * j + 1))
                before = xT[m] if j == 0 else hT[m]
                dve.scalar_tensor_tensor(hT[m][:, half(h)], FB[h][m][:], fb[:, 2 * j + 1, m:m + 1],
                                         before[:, half(h)], ALU.add, ALU.add).then_inc(h_ready[h], 1)

            def kv_bias(i, t, first, last):
                r, n = rotating(i, ("kv", t), last)
                dve.wait_ge(rot_full[r], n + 1)
                if t >= HT:
                    dve.wait_ge(kvt_done, nth(i, NT, t - HT))
                elif not first:
                    dve.wait_ge(kvt_done, nth(i - 1, NT, t + HT))
                dve.tensor_tensor(KV[:, t % HT, :], RB[r][:], kvb[:], ALU.add).then_inc(kv_ready, 1)

            def k_elu(i, t):
                dve.wait_ge(e_ready, nth(i, NT, t))
                dve.scalar_tensor_tensor(K[:, t % HT, :], E[:, t % HT, :], 1.0, KV[:, t % HT, 0:D],
                                         ALU.min, ALU.max).then_inc(k_ready, 1)

            def k_sum(i, t):
                dve.wait_ge(ks_ready, nth(i, NT, t))
                dve.tensor_reduce(ss[:, t % HT, :], E[:, t % HT, :].rearrange("p (h d) -> p h d", d=DEPTH),
                                  AX_X, ALU.add).then_inc(ss_ready, 1)

            def k_sum_eps(i, h):
                dve.wait_ge(ss_ready, nth(i, NT, h * HT + HT - 1))
                dve.tensor_scalar(sse[:], ss[:].rearrange("p t h -> p (t h)"), EPS_ATTN, None, ALU.add
                                  ).then_inc(sse_ready, 1)

            def k_newton(i, h):
                dve.wait_ge(r0_ready, nth(i, 2, h))
                dve.tensor_tensor(ra[:], r0[:], r0[:], ALU.mult).then_inc(ra_ready, 1)
                dve.wait_ge(ra_ready, nth(i, 2, h))
                dve.scalar_tensor_tensor(rc[:], ra[:], -0.5, sse[:], ALU.mult, ALU.mult).then_inc(rc_ready, 1)
                dve.wait_ge(rc_ready, nth(i, 2, h))
                dve.scalar_tensor_tensor(rk[:].rearrange("p t h -> p (t h)"), rc[:], 1.5, r0[:], ALU.add, ALU.mult
                                         ).then_inc(rk_ready, 1)

            def k_hat(i, t):
                dve.wait_ge(rk_ready, nth(i, 2, t // HT))
                dve.tensor_tensor(K[:, t % HT, :].rearrange("p (h d) -> p h d", d=DEPTH),
                                  K[:, t % HT, :].rearrange("p (h d) -> p h d", d=DEPTH),
                                  rk[:, t % HT, :].unsqueeze(2).broadcast_to([P, NH, DEPTH]), ALU.mult
                                  ).then_inc(kh_ready, 1)

            def q_min(i, h, m):
                dve.wait_ge(eq_ready, nth(i, 2 * NC, h * NC + m))
                dve.tensor_scalar(eq[:, m, :], eq[:, m, :], 1.0, None, ALU.min).then_inc(eq_min, 1)

            def q_elu(i, h, m, last):
                r, n = rotating(i, ("q", h, m), last)
                dve.wait_ge(eq_min, nth(i, 2 * NC, h * NC + m))
                dve.scalar_tensor_tensor(qT[m][:, half(h)], RB[r][:], bq1[:, m:m + 1], eq[:, m, :],
                                         ALU.add, ALU.max).then_inc(q_ready, 1)

            def block_diagonal(i):
                dve.wait_ge(kvt_done, nth(i, NT, NT - 1))
                dve.tensor_tensor(BD[:].rearrange("p (c n) -> p c n", c=NC),
                                  AB[:, 0:NC * P].rearrange("p (c n) -> p c n", c=NC),
                                  head_mask[:].unsqueeze(1).broadcast_to([P, NC, P]), ALU.mult).then_inc(bd_ready, 1)

            def att_y(i, p, last):
                r, n = rotating(i, ("out", p), last)
                dve.wait_ge(rot_full[r], n + 1)
                dve.wait_ge(xn_based, nth(i, 2, p // 2))
                if p >= 2:
                    dve.wait_ge(res_ready, nth(i, NT, 2 * p - 3))
                dve.tensor_tensor(Y[:, p % 2].rearrange("p t d -> p (t d)"), RB[r][:],
                                  XNB[:, 2 * p:2 * p + 2, :].rearrange("p t d -> p (t d)"), ALU.add
                                  ).then_inc(y_ready, 1)
                dve.wait_ge(y_ready, nth(i, NT // 2, p))
                for t in range(2):
                    dve.bn_stats(st2[:, 2 * p + t, :], Y[:, p % 2, t, :]).then_inc(ln2_stats, 1)
                dve.wait_ge(ln2_stats, nth(i, NT, 2 * p + 1))
                dve.sem_inc(stats_seen)
                for t in range(2):
                    dve.bn_aggr(mv2[:, 2 * p + t, :], st2[:, 2 * p + t, :]).then_inc(ln2_mean, 1)
                dve.wait_ge(ln2_mean, nth(i, NT, 2 * p + 1))
                dve.tensor_scalar(ve2[:, 2 * p:2 * p + 2], mv2[:, 2 * p:2 * p + 2, 1], EPS_ATTN, None, ALU.add
                                  ).then_inc(ln2_var, 1)

            def att_result(i, p):
                dve.wait_ge(x_based, nth(i, 2, p // 2))
                for t in range(2):
                    dve.scalar_tensor_tensor(Y[:, p % 2, t, :], Y[:, p % 2, t, :], mv2[:, 2 * p + t, 0:1], gamma_r[:],
                                             ALU.subtract, ALU.mult).then_inc(z_ready, 1)
                dve.wait_ge(ln2_rstd, nth(i, NT // 2, p))
                for t in range(2):
                    n = 2 * p + t
                    dve.wait_ge(z_ready, nth(i, NT, n))
                    dve.scalar_tensor_tensor(RES[:, n, :], Y[:, p % 2, t, :], rs2[:, n:n + 1], RES[:, n, :],
                                             ALU.mult, ALU.add).then_inc(res_ready, 1)

            def finish(i, p, last):
                r, n = rotating(i, ("fin", p), last)
                dve.wait_ge(rot_full[r], n + 1)
                dve.wait_ge(res_ready, nth(i, NT, 2 * p + 1))
                pair = RES[:, 2 * p:2 * p + 2, :].rearrange("p t d -> p (t d)")
                dve.tensor_tensor(pair, RB[r][:], pair, ALU.add).then_inc(o_ready, 1)

            for h in range(2):
                ln1_statistics(0, h)
                ln1_mean_var(0, h)
            for h in range(2):
                ln1_normalise(0, h, ahead=True)

            dve.wait_ge(w_row, 96)
            dve.wait_ge(w_col, 64)
            dve.tensor_scalar(bq1[:], bqc[:], 1.0, None, ALU.add).then_inc(vecs_ready, 1)
            chained(dve.tensor_reduce(b1m[:], b1_r[:], AX_X, ALU.add))
            chained(dve.tensor_scalar(b1m[:], b1m[:], -1.0 / D, None, ALU.mult))
            for j in range(NBLK):
                dve.tensor_scalar(b1c[:, j, :], fb[:, 2 * j, :], b1m[:, j:j + 1], None, ALU.add
                                  ).then_inc(vecs_ready, 1)
            dve.tensor_scalar(kvb[:, 0:D], kvb[:, 0:D], 1.0, None, ALU.add).then_inc(vecs_ready, 1)

            dve.wait_ge(w_q, 16 * NL)
            dve.wait_ge(w_sc, 16)
            dve.wait_ge(lbT_full, 1)
            for n in range(3):
                dve.tensor_copy(qT[n // 2][0:R, n % 2 * BANK:(n % 2 + 1) * BANK], bank[n][0:R, :]).then_inc(lbT_ready, 1)

            def dequantise(l):
                w = w_od[:, l % 2, :]
                if l >= 2:
                    dve.wait_ge(wT_full, l - 1)
                chained(dve.tensor_scalar(w, q_int[l], 1.0 / 7.5, -1.0,
                                          ALU.mult, ALU.add))
                chained(dve.tensor_tensor(w.rearrange("p (g e) -> p g e", e=GROUP),
                                          w.rearrange("p (g e) -> p g e", e=GROUP),
                                          sc[:, l].rearrange("p c g -> p (c g)").unsqueeze(2)
                                          .broadcast_to([P, NC * NG, GROUP]), ALU.mult))
                dve.wait_ge(lora_full, l + 1)
                dve.tensor_tensor(w, w, bank[2 + l % 2][:], ALU.add).then_inc(w_od_ready, 1)

            def centre(l):
                b = bank[1]
                dve.wait_ge(wT_full, l + 1)
                chained(dve.tensor_reduce(wmean[:, 0, :], b[:].rearrange("p (c d) -> p c d", c=NC), AX_X, ALU.add))
                chained(dve.tensor_scalar(wmean[:, 1, :], wmean[:, 0, :], -1.0 / D, None, ALU.mult))
                for c in range(NC):
                    dve.tensor_scalar(WT[:, 0, c, :], b[:, c * D:(c + 1) * D], wmean[:, 1, c:c + 1], None,
                                      ALU.add).then_inc(wT_centred, 1)

            def split_low(l):
                dve.wait_ge(wT_high, l + 1)
                dve.tensor_tensor(WTl[:, l], WT[:, l % 2], WTh[:, l].bitcast(F32), ALU.subtract).then_inc(wT_split, 1)

            dve.wait_ge(vecs_ready, NBLK + 2)
            dve.wait_ge(consts, 5)
            for l in range(NL):
                dequantise(l)
                if l % 2 == 0:
                    if l:
                        dve.wait_ge(wT_split, l - 1)
                    centre(l)
                if l == 1:
                    for h in range(2):
                        for c in range(NC):
                            xt_low(0, h, c)
                    dve.wait_ge(wkvq_high, 2)
                    dve.tensor_tensor(Wkvl[:], Wkv[:], Wkvh[:].bitcast(F32), ALU.subtract).then_inc(wkvq_split, 1)
                    dve.tensor_tensor(Wql[:], Wqs[:], Wqh[:].bitcast(F32), ALU.subtract).then_inc(wkvq_split, 1)
                if l:
                    split_low(l - 1)
            split_low(NL - 1)

            def body(i, first, last):
                kv_bias(i, 0, first, last)
                ffn_var(i, 0, 0, last)
                kv_bias(i, 1, first, last)
                ffn_normalise(i, 0, 0, 0)
                ffn_normalise(i, 0, 0, 1)
                k_elu(i, 0)
                ffn_var(i, 1, 0, last)
                kv_bias(i, 2, first, last)
                if not last:
                    ln1_statistics(i + 1, 0)
                    ln1_mean_var(i + 1, 0)
                k_elu(i, 1)
                ffn_normalise(i, 1, 0, 0)
                ffn_normalise(i, 1, 0, 1)
                g_lower(dve, i, 0, 0, 0)
                g_lower(dve, i, 0, 0, 1)
                g_lower(dve, i, 1, 0, 0)
                ffn_residual(i, 0, 0, 0)
                ffn_residual(i, 0, 0, 1)
                kv_bias(i, 3, first, last)
                if not last:
                    ln1_statistics(i + 1, 1)
                    ln1_mean_var(i + 1, 1)
                ffn_residual(i, 1, 0, 0)
                k_elu(i, 2)
                k_elu(i, 3)
                k_sum(i, 0)
                ffn_residual(i, 1, 0, 1)
                k_sum(i, 1)
                k_sum(i, 2)
                h_lower(dve, i, 1, 0, 0)
                k_sum(i, 3)
                k_sum_eps(i, 0)
                h_lower(dve, i, 1, 0, 1)
                k_newton(i, 0)
                k_hat(i, 0)
                k_hat(i, 1)
                ffn_var(i, 0, 1, last)
                k_hat(i, 2)
                kv_bias(i, 4, first, last)
                k_hat(i, 3)
                kv_bias(i, 5, first, last)
                ffn_normalise(i, 0, 1, 0)
                ffn_normalise(i, 0, 1, 1)
                ffn_var(i, 1, 1, last)
                kv_bias(i, 6, first, last)
                ffn_normalise(i, 1, 1, 0)
                ffn_normalise(i, 1, 1, 1)
                k_elu(i, 4)
                g_lower(dve, i, 0, 1, 0)
                kv_bias(i, 7, first, last)
                g_lower(dve, i, 1, 1, 0)
                k_elu(i, 5)
                g_lower(dve, i, 1, 1, 1)
                k_sum(i, 4)
                ffn_residual(i, 0, 1, 0)
                ffn_residual(i, 0, 1, 1)
                if not last:
                    ln1_normalise(i + 1, 0)
                q_min(i, 0, 0)
                k_elu(i, 6)
                ffn_residual(i, 1, 1, 0)
                k_elu(i, 7)
                k_sum(i, 5)
                k_sum(i, 6)
                k_sum(i, 7)
                k_sum_eps(i, 1)
                q_elu(i, 0, 0, last)
                h_lower(dve, i, 1, 1, 0)
                ffn_residual(i, 1, 1, 1)
                k_newton(i, 1)
                q_min(i, 0, 1)
                k_hat(i, 4)
                h_lower(dve, i, 1, 1, 1)
                q_elu(i, 0, 1, last)
                k_hat(i, 5)
                q_min(i, 1, 0)
                k_hat(i, 6)
                k_hat(i, 7)
                q_elu(i, 1, 0, last)
                ffn_var(i, 0, 2, last)
                q_min(i, 1, 1)
                q_elu(i, 1, 1, last)
                block_diagonal(i)
                if not last:
                    ln1_normalise(i + 1, 1)
                ffn_normalise(i, 0, 2, 0)
                ffn_var(i, 1, 2, last)
                if not last:
                    xt_low(i + 1, 0, 0)
                ffn_normalise(i, 0, 2, 1)
                att_y(i, 0, last)
                ffn_normalise(i, 1, 2, 0)
                ffn_normalise(i, 1, 2, 1)
                att_result(i, 0)
                att_y(i, 1, last)
                att_y(i, 2, last)
                ffn_residual(i, 0, 2, 0)
                ffn_residual(i, 0, 2, 1)
                att_result(i, 1)
                finish(i, 0, last)
                ffn_residual(i, 1, 2, 0)
                finish(i, 1, last)
                ffn_residual(i, 1, 2, 1)
                if not last:
                    xt_low(i + 1, 0, 1)
                att_y(i, 3, last)
                att_result(i, 2)
                if not last:
                    xt_low(i + 1, 1, 0)
                    xt_low(i + 1, 1, 1)
                att_result(i, 3)
                finish(i, 2, last)
                finish(i, 3, last)

            batches(dve, body)

        @block.tensor
        def _(pe):
            def read_by(i, use):
                kind, *at = use
                return {
                    "var": lambda h, j: (fvar_ready[h], nth(i, NBLK, j)),
                    "rs": lambda h, j: (rb_ready[h], nth(i, NBLK, j)),
                    "kv": lambda t: (kv_ready, nth(i, NT, t)),
                    "q": lambda h, m: (q_ready, nth(i, 2 * NC, h * NC + m)),
                    "out": lambda p: (y_ready, nth(i, NT // 2, p)),
                    "xt": lambda h, c: (xT_ready, nth(i + 1, 2 * NC, h * NC + c)),
                    "fin": lambda p: (o_ready, nth(i, NT // 2, p)),
                }[kind](*at)

            def take(i, use, first, last):
                now = bank_uses(last)
                n = now.index(use)
                if n >= NROT:
                    before = read_by(i, now[n - NROT])
                elif first:
                    before = (xT_ready, AHEAD + n - NROT + 1)
                else:
                    before = read_by(i - 1, bank_uses(False)[n - NROT])
                pe.wait_ge(*before)
                return rotating(i, use, last)[0]

            def xt(b, h, c, last, ahead=False):
                if not ahead:
                    r = take(b - 1, ("xt", h, c), False, last)
                else:
                    r = (h * NC + c) % NROT
                    if h * NC + c >= NROT:
                        pe.wait_ge(xT_ready, h * NC + c - NROT + 1)
                pe.wait_ge(xn_ready, nth(b, NT, h * HT + HT - 1))
                for t in range(HT):
                    ins = pe.transpose(RB[r][:, t * P:(t + 1) * P], XN[:, h * HT + t, c * P:(c + 1) * P], ident[:])
                ins.then_inc(rot_full[r], 1)

            def high_products(l, h, k, high):
                for n, w in enumerate((WTl, WTh)):
                    for m in range(NC):
                        pe.matmul(FB[h][m][:], w[:, l, k, m * P:(m + 1) * P], high, start=(k == 0 and n == 0),
                                  stop=False)

            def low_products(l, h, k, low):
                for m in range(NC):
                    ins = pe.matmul(FB[h][m][:], WTh[:, l, k, m * P:(m + 1) * P], low, start=False,
                                    stop=(k == NC - 1))
                    if k == NC - 1:
                        ins.then_inc(ffn_full[h][m], 1)

            def first_linear(i, h, j):
                if j == 0:
                    for k in range(NC):
                        pe.wait_ge(xT_high, nth(i, 2 * NC, h * NC + k))
                        high_products(0, h, k, xTh[k][:, half(h)])
                    for k in range(NC):
                        pe.wait_ge(xT_low, nth(i, 2 * NC, h * NC + k))
                        low_products(0, h, k, xTl[k][:, half(h)])
                else:
                    pe.wait_ge(h_ready[h], nth(i, NBLK * NC, j * NC - 1))
                    for k in range(NC):
                        pe.wait_ge(h_high[h], nth(i, (NBLK - 1) * NC, (j - 1) * NC + k))
                        high_products(2 * j, h, k, hTh[k][:, half(h)])
                    for k in range(NC):
                        pe.wait_ge(h_low[h][k], nth(i, NBLK - 1, j - 1))
                        low_products(2 * j, h, k, hTl[k][:, half(h)])

            def second_linear(i, h, j):
                pe.wait_ge(yn_ready[h], nth(i, NBLK * NC, j * NC + NC - 1))
                for k in range(NC):
                    pe.wait_ge(g_high[h], nth(i, NBLK * NC, j * NC + k))
                    high_products(2 * j + 1, h, k, gh[:, h, k, :])
                for k in range(NC):
                    pe.wait_ge(g_low[h][k], nth(i, NBLK, j))
                    low_products(2 * j + 1, h, k, gl[:, h, k, :])

            def variance(i, h, j, first, last):
                r = take(i, ("var", h, j), first, last)
                pe.wait_ge(sqs_ready[h], nth(i, NBLK, j))
                for t in range(HT):
                    ins = pe.matmul(RB[r][:, t * P:(t + 1) * P], sqs[:, h, t * P:(t + 1) * P], mean_w[:],
                                    start=True, stop=True)
                ins.then_inc(rot_full[r], 1)

            def spread_rstd(i, h, j, first, last):
                r = take(i, ("rs", h, j), first, last)
                pe.wait_ge(frstd_ready[h], nth(i, NBLK, j))
                for t in range(HT):
                    ins = pe.transpose(RB[r][:, t * P:(t + 1) * P], rsf[:, h, t:t + 1].broadcast_to([P, P]), ident[:])
                ins.then_inc(rot_full[r], 1)

            def xt_parts_there(i, h):
                pe.wait_ge(xT_high, nth(i, 2 * NC, h * NC + NC - 1))
                pe.wait_ge(xT_low, nth(i, 2 * NC, h * NC + NC - 1))

            def project_kv(i, t, first, last):
                r = take(i, ("kv", t), first, last)
                if t % HT == 0:
                    xt_parts_there(i, t // HT)
                pairs = [(x, w, k) for x, w in ((xTh, Wkvl), (xTh, Wkvh), (xTl, Wkvh)) for k in range(NC)]
                for n, (x_, w, k) in enumerate(pairs):
                    ins = pe.matmul(RB[r][:], x_[k][:, t * P:(t + 1) * P], w[:, k, :],
                                    start=(n == 0), stop=(n == len(pairs) - 1))
                ins.then_inc(rot_full[r], 1)

            def add_vk(i, t, first):
                pe.wait_ge(kh_ready, nth(i, NT, t))
                if t == 0 and not first:
                    pe.wait_ge(m_ready, nth(i - 1, 1, 0))
                for c in range(NC):
                    ins = pe.matmul(AB[:, c * P:(c + 1) * P], KV[:, t % HT, D + c * P:D + (c + 1) * P],
                                    K[:, t % HT, c * P:(c + 1) * P], start=(t == 0 and c == 0),
                                    stop=(t == NT - 1), skip_group_check=True)
                ins.then_inc(kvt_done, 1)

            def project_q(i, h, m, first, last):
                r = take(i, ("q", h, m), first, last)
                if m == 0:
                    xt_parts_there(i, h)
                pairs = [(w, x, k) for w, x in ((Wql, xTh), (Wqh, xTh), (Wqh, xTl)) for k in range(NC)]
                for n, (w, x_, k) in enumerate(pairs):
                    ins = pe.matmul(RB[r][:], w[:, k, m * P:(m + 1) * P], x_[k][:, half(h)],
                                    start=(n == 0), stop=(n == len(pairs) - 1))
                ins.then_inc(rot_full[r], 1)

            def make_m(i):
                pe.wait_ge(bd_ready, nth(i, 1, 0))
                for c in range(NC):
                    ins = pe.matmul(AB[:, c * D:(c + 1) * D], BD[:, c * P:(c + 1) * P], Wos[:, c, :],
                                    start=True, stop=True)
                ins.then_inc(m_full, 1)

            def attend(i, p, first, last):
                r = take(i, ("out", p), first, last)
                pe.wait_ge(q_ready, nth(i, 2 * NC, p // 2 * NC + NC - 1))
                pe.wait_ge(m_ready, nth(i, 1, 0))
                for t in range(2):
                    for c in range(NC):
                        ins = pe.matmul(RB[r][:, t * D:(t + 1) * D], qT[c][:, (2 * p + t) * P:(2 * p + t + 1) * P],
                                        M[:, c, :], start=(c == 0), stop=(c == NC - 1))
                ins.then_inc(rot_full[r], 1)

            def to_rows(i, p, first, last):
                r = take(i, ("fin", p), first, last)
                pe.wait_ge(h_ready[p // 2], nth(i, NBLK * NC, NBLK * NC - 1))
                for t in range(2):
                    for c in range(NC):
                        ins = pe.transpose(RB[r][:, t * D + c * P:t * D + (c + 1) * P],
                                           hT[c][:, (2 * p + t) * P:(2 * p + t + 1) * P], ident[:])
                ins.then_inc(rot_full[r], 1)

            pe.wait_ge(consts, 5)
            for h in range(2):
                for c in range(NC):
                    xt(0, h, c, False, ahead=True)
            pe.wait_ge(w_lb, 16)
            for n in range(NL * NC):
                ins = pe.transpose(bank[n // 4][0:R, n % 4 * P:(n % 4 + 1) * P], lb[:, n // NC, n % NC, :], ident[:])
            ins.then_inc(lbT_full, 1)
            pe.wait_ge(w_la, 16 * NL)
            pe.wait_ge(lbT_ready, 3)
            for l in range(NL + 1):
                if l < NL:
                    if l >= 2:
                        pe.wait_ge(w_od_ready, l - 1)
                    for c in range(NC):
                        n = l * NC + c
                        ins = pe.matmul(bank[2 + l % 2][:, c * D:(c + 1) * D], lbT(n), la[l],
                                        start=True, stop=True)
                    ins.then_inc(lora_full, 1)
                if l >= 1:
                    m = l - 1
                    pe.wait_ge(w_od_ready, m + 1)
                    if m >= 2:
                        if m % 2 == 0:
                            pe.wait_ge(wT_centred, NC * (m // 2))
                        else:
                            pe.wait_ge(wT_copied, m // 2)
                    for k in range(NC):
                        for c in range(NC):
                            ins = pe.transpose(bank[(1, 4)[m % 2]][:, k * D + c * P:k * D + (c + 1) * P],
                                               w_od[:, m % 2, c * D + k * P:c * D + (k + 1) * P], ident[:])
                    ins.then_inc(wT_full, 1)
            pe.wait_ge(wT_split, NL)
            pe.wait_ge(wkvq_split, 2)
            pe.wait_ge(w_qkvo, 64)

            def body(i, first, last):
                first_linear(i, 0, 0)
                first_linear(i, 1, 0)
                project_kv(i, 0, first, last)
                variance(i, 0, 0, first, last)
                project_kv(i, 1, first, last)
                spread_rstd(i, 0, 0, first, last)
                project_kv(i, 2, first, last)
                variance(i, 1, 0, first, last)
                project_kv(i, 3, first, last)
                spread_rstd(i, 1, 0, first, last)
                project_kv(i, 4, first, last)
                second_linear(i, 0, 0)
                second_linear(i, 1, 0)
                first_linear(i, 0, 1)
                project_kv(i, 5, first, last)
                first_linear(i, 1, 1)
                variance(i, 0, 1, first, last)
                add_vk(i, 0, first)
                add_vk(i, 1, first)
                add_vk(i, 2, first)
                spread_rstd(i, 0, 1, first, last)
                add_vk(i, 3, first)
                project_kv(i, 6, first, last)
                variance(i, 1, 1, first, last)
                project_kv(i, 7, first, last)
                spread_rstd(i, 1, 1, first, last)
                project_q(i, 0, 0, first, last)
                second_linear(i, 0, 1)
                second_linear(i, 1, 1)
                project_q(i, 0, 1, first, last)
                project_q(i, 1, 0, first, last)
                first_linear(i, 0, 2)
                project_q(i, 1, 1, first, last)
                first_linear(i, 1, 2)
                add_vk(i, 4, first)
                add_vk(i, 5, first)
                variance(i, 0, 2, first, last)
                add_vk(i, 6, first)
                add_vk(i, 7, first)
                if not last:
                    xt(i + 1, 0, 0, last)
                spread_rstd(i, 0, 2, first, last)
                make_m(i)
                variance(i, 1, 2, first, last)
                attend(i, 0, first, last)
                spread_rstd(i, 1, 2, first, last)
                if not last:
                    xt(i + 1, 0, 1, last)
                attend(i, 1, first, last)
                if not last:
                    xt(i + 1, 1, 0, last)
                attend(i, 2, first, last)
                second_linear(i, 0, 2)
                second_linear(i, 1, 2)
                to_rows(i, 0, first, last)
                if not last:
                    xt(i + 1, 1, 1, last)
                to_rows(i, 1, first, last)
                attend(i, 3, first, last)
                to_rows(i, 2, first, last)
                to_rows(i, 3, first, last)

            batches(pe, body)


_INS = ["L0_attn_x", "L0_attn_Wq", "L0_attn_bq", "L0_attn_Wk", "L0_attn_bk", "L0_attn_Wv", "L0_attn_bv",
        "L0_attn_Wo", "L0_attn_bo", "L0_attn_gamma", "L0_attn_beta", "L0_ffn_qweights", "L0_ffn_scales",
        "L0_ffn_biases", "L0_ffn_lora_a", "L0_ffn_lora_b", "L0_ffn_ln_gamma", "L0_ffn_ln_beta"]
_OUTS = [((8, 1024, 256), "float32")]


def kernel(**inputs):
    import numpy as _np
    import concourse.bacc as _bacc
    from concourse import mybir as _mybir
    from concourse.bass_utils import run_bass_kernel_spmd as _run

    nc = _bacc.Bacc("TRN2", target_bir_lowering=False, num_devices=1)
    arrays, args = {}, []
    for name in _INS:
        a = _np.ascontiguousarray(inputs[name])
        arrays[f"in_{name}_dram"] = a
        args.append(nc.dram_tensor(f"in_{name}_dram", a.shape, _mybir.dt.from_np(a.dtype), kind="ExternalInput").ap())
    for i, (shape, dtype) in enumerate(_OUTS):
        dt = _mybir.dt.from_np(_np.dtype(dtype))
        args.append(nc.dram_tensor(f"out_{i}_dram", shape, dt, kind="ExternalOutput").ap())
    block_kernel(nc, *args)
    r = _run(nc, [arrays], core_ids=[0])
    got = tuple(r.results[0][f"out_{i}_dram"] for i in range(len(_OUTS)))
    return got[0]
```

```python
from contextlib import ExitStack

import concourse.bass as bass
from concourse import mybir

ALU = mybir.AluOpType
ACT = mybir.ActivationFunctionType
F32 = mybir.dt.float32
I32 = mybir.dt.int32
F32R = mybir.dt.float32r
AX_X = mybir.AxisListType.X

P = 128
BANK = 512
NT = 8
HT = NT // 2
NBLK = 3
DEPTH = 16
GROUP = 16
EPS_LN = 1e-5
EPS_ATTN = 1e-6
GUESS_BITS = float(0x5f3759df)
NEWTON = 3

def bank_uses(last):
    uses = [
        ("kv", 0), ("var", 0, 0), ("kv", 1), ("var", 1, 0), ("rs", 0, 0), ("kv", 2), ("kv", 3), ("rs", 1, 0),
        ("kv", 4), ("kv", 5), ("kv", 6), ("var", 0, 1), ("kv", 7), ("var", 1, 1), ("rs", 0, 1), ("rs", 1, 1),
        ("q", 0, 0), ("q", 0, 1), ("q", 1, 0), ("xt", 0, 0), ("q", 1, 1), ("var", 0, 2), ("xt", 0, 1),
        ("rs", 0, 2), ("out", 0), ("out", 1), ("var", 1, 2), ("xt", 1, 0), ("rs", 1, 2), ("xt", 1, 1),
        ("out", 2), ("fin", 0), ("fin", 1), ("out", 3), ("fin", 2), ("fin", 3)
    ]
    return [use for use in uses if not (last and use[0] == "xt")]


USES = len(bank_uses(False))
NROT = 3
AHEAD = 4
assert USES % NROT == 0


def rotating(i, use, last):
    n = AHEAD + bank_uses(last).index(use)
    return n % NROT, i * (USES // NROT) + n // NROT


def nth(i, per, n):
    return i * per + (n + 1)


def block_kernel(nc: bass.Bass, x, Wq, bq, Wk, bk, Wv, bv, Wo, bo, gamma, beta,
                 qweights, scales, biases, lora_a, lora_b, ln_gamma, ln_beta, out):
    NB, S, D = x.shape
    NL = qweights.shape[0]
    R = lora_a.shape[1]
    NC = D // P
    NG = D // GROUP
    NH = D // DEPTH
    assert S == NT * P and NC == 2 and NL == 2 * NBLK and D == 256

    x_rows = x.rearrange("b (p t) d -> b p t d", t=NT)
    out_rows = out.rearrange("b (p t) d -> b p t d", t=NT)

    ctx = ExitStack()
    with ctx:
        def sb(name, shape, dt=F32):
            return ctx.enter_context(nc.sbuf_tensor(name, shape, dt))

        def sem(name):
            return ctx.enter_context(nc.semaphore(name))

        sc = sb("sc", [P, NL, NC, NG])
        lb = sb("lb", [P, NL, NC, R])
        WTh = sb("WTh", [P, NL, NC, D], F32R)
        WTl = sb("WTl", [P, NL, NC, D], F32R)
        Wqs = sb("Wqs", [P, NC, D])
        Wqh = sb("Wqh", [P, NC, D], F32R)
        Wql = sb("Wql", [P, NC, D], F32R)
        Wkv = sb("Wkv", [P, NC, 2 * D])
        Wkvh = sb("Wkvh", [P, NC, 2 * D], F32R)
        Wkvl = sb("Wkvl", [P, NC, 2 * D], F32R)
        Wos = sb("Wos", [P, NC, D])
        ident = sb("ident", [P, P])
        head_mask = sb("head_mask", [P, P])
        mean_w = sb("mean_w", [P, P])
        neg1 = sb("neg1", [P, 1])
        neghalf = sb("neghalf", [P, HT])
        kvb = sb("kvb", [P, 2 * D])
        bo_r = sb("bo_r", [P, D])
        gamma_r = sb("gamma_r", [P, D])
        beta_r = sb("beta_r", [P, D])
        b1_r = sb("b1_r", [P, NBLK, D])
        fb = sb("fb", [P, NL, NC])
        lng = sb("lng", [P, NBLK, NC])
        lnb = sb("lnb", [P, NBLK, NC])
        bqc = sb("bqc", [P, NC])
        bq1 = sb("bq1", [P, NC])
        b1c = sb("b1c", [P, NBLK, NC])
        b1m = sb("b1m", [P, NBLK])
        wmean = sb("wmean", [P, 2, NC])
        X = sb("X", [P, NT, D])
        XN = sb("XN", [P, NT, D])
        XNB = sb("XNB", [P, NT, D])
        RES = sb("RES", [P, NT, D])
        xT = [sb(f"xT{c}", [P, S]) for c in range(NC)]
        hT = [sb(f"hT{c}", [P, S]) for c in range(NC)]
        xTh, xTl, hTh, hTl = ([sb(f"{n}{c}", [P, S], F32R) for c in range(NC)] for n in ("xTh", "xTl", "hTh", "hTl"))
        qT = [sb(f"qT{c}", [P, S]) for c in range(NC)]

        def lbT(n):
            return qT[n // NT][0:R, n % NT * P:(n % NT + 1) * P]

        st1 = sb("st1", [P, NT, 6])
        mv1 = sb("mv1", [P, NT, 2])
        ve1 = sb("ve1", [P, NT])
        rs1 = sb("rs1", [P, NT])
        st2 = sb("st2", [P, NT, 6])
        mv2 = sb("mv2", [P, NT, 2])
        ve2 = sb("ve2", [P, NT])
        rs2 = sb("rs2", [P, NT])
        fw = sb("fw", [P, 2, NC, BANK])
        sqs = sb("sqs", [P, 2, BANK])
        vef = sb("vef", [P, 2, HT])
        rsf = sb("rsf", [P, 2, HT])
        w_od = [fw[:, l // 2, l % 2, :] for l in range(4)]
        w_od += [hT[0][:, l * NC * D:(l + 1) * NC * D] for l in range(2)]
        rb = sb("rb", [P, 2, BANK])
        gh = sb("gh", [P, 2, NC, BANK], F32R)
        gl = sb("gl", [P, 2, NC, BANK], F32R)
        KV = sb("KV", [P, HT, 2 * D])
        E = sb("E", [P, HT, D])
        K = sb("K", [P, HT, D])
        ss = sb("ss", [P, HT, NH])
        sse = sb("sse", [P, HT * NH])
        guess = sb("guess", [P, HT * NH])
        guess_sq = sb("guess_sq", [P, HT * NH])
        guess_off = sb("guess_off", [P, HT * NH])
        rk = sb("rk", [P, HT, NH])
        eq = sb("eq", [P, NC, BANK])
        la_a, la_b = hT[1][0:R, :], eq[0:R, 0, :]
        la = [la_a[:, l * D:(l + 1) * D] for l in range(4)] + [la_b[:, l * D:(l + 1) * D] for l in range(2)]
        BD = sb("BD", [P, NC * P])
        M = sb("M", [P, NC, D])
        Y = sb("Y", [P, 2, 2, D])
        WT = [buf[:, s * NC:(s + 1) * NC, :] for buf in (E, K) for s in range(2)]

        bank = [ctx.enter_context(nc.psum_tensor(f"bank{n}", [P, BANK], F32)) for n in range(8)]
        FB = [bank[0:2], bank[2:4]]
        AB = bank[4]
        RB = bank[5:8]

        w_sc, w_la, w_lb, w_qkvo, w_row, w_col = (
            sem(n) for n in ("w_sc", "w_la", "w_lb", "w_qkvo", "w_row", "w_col"))
        w_q = [sem(f"w_q{g}") for g in range(NBLK)]
        w_unscaled = sem("w_unscaled")
        w_scaled = sem("w_scaled")
        consts = sem("consts")
        consts_step = sem("consts_step")
        dve_prep = sem("dve_prep")
        lbT_full = sem("lbT_full")
        lbT_ready = sem("lbT_ready")
        lora_full = sem("lora_full")
        w_od_ready = sem("w_od_ready")
        wT_full = sem("wT_full")
        wmean_ready = sem("wmean_ready")
        wT_made = sem("wT_made")
        wT_high = sem("wT_high")
        wT_split = sem("wT_split")
        wkvq_high = sem("wkvq_high")
        wkvq_split = sem("wkvq_split")
        xT_high, xT_low = sem("xT_high"), sem("xT_low")
        g_high, h_high = ([sem(f"{n}{h}") for h in range(2)] for n in ("g_high", "h_high"))
        g_low, h_low = ([[sem(f"{n}{h}{m}") for m in range(NC)] for h in range(2)] for n in ("g_low", "h_low"))
        vecs_ready = sem("vecs_ready")
        x_loaded = [sem(f"x_loaded{h}") for h in range(2)]
        x_based = sem("x_based")
        xn_based = sem("xn_based")
        ln1_stats, ln1_mean, ln1_var, ln1_rstd, xn_ready = (
            sem(n) for n in ("ln1_stats", "ln1_mean", "ln1_var", "ln1_rstd", "xn_ready"))
        stats_seen = sem("stats_seen")
        xT_ready = sem("xT_ready")
        rot_full = [sem(f"rot_full{n}") for n in range(NROT)]
        ffn_full = [[sem(f"ffn_full{h}{m}") for m in range(NC)] for h in range(2)]
        m_full = sem("m_full")
        sq_ready, sqs_ready, fvar_ready, frstd_ready, rb_ready, yn_ready, g_ready, h_ready = (
            [sem(f"{n}{h}") for h in range(2)]
            for n in ("sq_ready", "sqs_ready", "fvar_ready", "frstd_ready", "rb_ready", "yn_ready", "g_ready",
                      "h_ready"))
        kv_ready, e_ready, k_ready, ks_ready, ss_ready, sse_ready, guess_ready, guess_sq_ready, \
            guess_off_ready, rk_ready, kh_ready, kvt_done = (sem(n) for n in (
                "kv_ready", "e_ready", "k_ready", "ks_ready", "ss_ready", "sse_ready", "guess_ready",
                "guess_sq_ready", "guess_off_ready", "rk_ready", "kh_ready", "kvt_done"))
        eq_ready, eq_min, q_ready, bd_ready, m_ready = (
            sem(n) for n in ("eq_ready", "eq_min", "q_ready", "bd_ready", "m_ready"))
        y_ready, ln2_stats, ln2_mean, ln2_var, ln2_rstd, z_ready, res_ready = (
            sem(n) for n in ("y_ready", "ln2_stats", "ln2_mean", "ln2_var", "ln2_rstd", "z_ready", "res_ready"))
        o_ready = sem("o_ready")
        stored = [sem(f"stored{h}") for h in range(2)]

        def half(h):
            return slice(h * BANK, (h + 1) * BANK)

        def batches(engine, body):
            body(0, True, False)
            with engine.Fori(1, NB - 1) as i:
                body(i, False, False)
            body(NB - 1, False, True)

        block = ctx.enter_context(nc.Block())

        def g_lower(engine, i, h, j, m):
            engine.wait_ge(g_high[h], nth(i, NBLK * NC, j * NC + m))
            engine.tensor_tensor(gl[:, h, m, :], fw[:, h, m, :], gh[:, h, m, :].bitcast(F32), ALU.subtract
                                 ).then_inc(g_low[h][m], 1)

        def xt_lower(engine, b, h, c):
            engine.wait_ge(xT_ready, nth(b, 2 * NC, h * NC + c))
            engine.tensor_tensor(xTl[c][:, half(h)], xT[c][:, half(h)], xTh[c][:, half(h)].bitcast(F32), ALU.subtract
                                 ).then_inc(xT_low, 1)

        def h_lower(engine, i, h, j, m):
            engine.wait_ge(h_high[h], nth(i, (NBLK - 1) * NC, j * NC + m))
            engine.tensor_tensor(hTl[m][:, half(h)], hT[m][:, half(h)], hTh[m][:, half(h)].bitcast(F32), ALU.subtract
                                 ).then_inc(h_low[h][m], 1)

        @block.sync
        def _(sp):
            def load_x(b, h):
                sp.dma_start(X[:, h * HT:(h + 1) * HT, :],
                             x_rows[bass.ds(b, 1), :, h * HT:(h + 1) * HT, :].rearrange("o p t d -> (o p) t d")
                             ).then_inc(x_loaded[h], 16)

            load_x(0, 0)
            load_x(0, 1)
            for dst, src in ((kvb[:, 0:D], bk), (kvb[:, D:], bv), (bo_r[:], bo), (gamma_r[:], gamma), (beta_r[:], beta)):
                sp.dma_start(dst, src.unsqueeze(0).broadcast_to([P, D])).then_inc(w_row, 16)
            sp.dma_start(b1_r[:], biases.rearrange("(j two) d -> two j d", two=2)[0:1]
                         .broadcast_to([P, NBLK, D])).then_inc(w_row, 16)
            with nc.allow_non_contiguous_dma(reason="short vectors, feature on the partition"):
                sp.dma_start(fb[:], biases.rearrange("l (c p) -> p l c", p=P)).then_inc(w_col, 16)
                sp.dma_start(lng[:], ln_gamma.rearrange("l (c p) -> p l c", p=P)).then_inc(w_col, 16)
                sp.dma_start(lnb[:], ln_beta.rearrange("l (c p) -> p l c", p=P)).then_inc(w_col, 16)
                sp.dma_start(bqc[:], bq.rearrange("(c p) -> p c", p=P)).then_inc(w_col, 16)

            def body(i, first, last):
                for h in range(2):
                    if not last:
                        sp.wait_ge(x_based, nth(i, 2, h))
                        load_x(i + 1, h)
                for h in range(2):
                    sp.wait_ge(o_ready, nth(i, NT // 2, 2 * h + 1))
                    sp.dma_start(out_rows[bass.ds(i, 1), :, h * HT:(h + 1) * HT, :].rearrange("o p t d -> (o p) t d"),
                                 RES[:, h * HT:(h + 1) * HT, :]).then_inc(stored[h], 16)

            batches(sp, body)
            for h in range(2):
                sp.wait_ge(stored[h], 16 * NB)

        @block.gpsimd
        def _(pool):
            pool.memset(ident[:], 0.0).then_inc(consts_step, 1)
            pool.memset(head_mask[:], 1.0).then_inc(consts_step, 1)
            pool.memset(mean_w[:], 1.0 / D).then_inc(consts, 1)
            pool.memset(neg1[:], -1.0).then_inc(consts, 1)
            pool.memset(neghalf[:], -0.5).then_inc(consts, 1)
            pool.wait_ge(consts_step, 2)
            pool.affine_select(out=ident[:], in_=ident[:], compare_op=ALU.not_equal, fill=1.0,
                               base=0, pattern=[[-1, P]], channel_multiplier=1).then_inc(consts, 1)
            heads = head_mask[:].rearrange("p (h d) -> p h d", d=DEPTH)
            pool.affine_select(out=heads, in_=heads, compare_op=ALU.is_ge, fill=0.0, base=0,
                               pattern=[[-DEPTH, P // DEPTH], [0, DEPTH]], channel_multiplier=1
                               ).then_inc(consts_step, 1)
            pool.wait_ge(consts_step, 3)
            pool.affine_select(out=heads, in_=heads, compare_op=ALU.is_ge, fill=0.0, base=DEPTH - 1,
                               pattern=[[DEPTH, P // DEPTH], [0, DEPTH]], channel_multiplier=-1).then_inc(consts, 1)

            def rstd(dst, var, n):
                return pool.tensor_tensor(dst, var, neghalf[:, 0:n], ALU.pow)

            def ln1_root(b, h):
                pool.wait_ge(ln1_var, nth(b, 2, h))
                rstd(rs1[:, h * HT:(h + 1) * HT], ve1[:, h * HT:(h + 1) * HT], HT).then_inc(ln1_rstd, 1)

            def base_x(i, h, first):
                pool.wait_ge(xn_ready, nth(i, NT, h * HT + HT - 1))
                if not first:
                    pool.wait_ge(stored[h], 16 * i)
                pool.tensor_tensor(RES[:, h * HT:(h + 1) * HT, :], X[:, h * HT:(h + 1) * HT, :],
                                   beta_r[:].unsqueeze(1).broadcast_to([P, HT, D]), ALU.add).then_inc(x_based, 1)

            def base_xn(i, h, first):
                pool.wait_ge(xn_ready, nth(i, NT, h * HT + HT - 1))
                if not first:
                    pool.wait_ge(y_ready, nth(i - 1, NT // 2, 2 * h + 1))
                pool.tensor_tensor(XNB[:, h * HT:(h + 1) * HT, :], XN[:, h * HT:(h + 1) * HT, :],
                                   bo_r[:].unsqueeze(1).broadcast_to([P, HT, D]), ALU.add).then_inc(xn_based, 1)

            def add_squares(i, h, j):
                pool.wait_ge(sq_ready[h], nth(i, NBLK * NC, j * NC + NC - 1))
                pool.tensor_tensor(sqs[:, h, :], fw[:, h, 0, :], fw[:, h, 1, :], ALU.add).then_inc(sqs_ready[h], 1)

            def ffn_root(i, h, j):
                pool.wait_ge(fvar_ready[h], nth(i, NBLK, j))
                rstd(rsf[:, h, :], vef[:, h, :], HT).then_inc(frstd_ready[h], 1)

            def ln2_root(i, p):
                pool.wait_ge(ln2_var, nth(i, NT // 2, p))
                rstd(rs2[:, 2 * p:2 * p + 2], ve2[:, 2 * p:2 * p + 2], 2).then_inc(ln2_rstd, 1)

            def dequantise(l):
                pool.wait_ge(w_q[l // 2], 16)
                pool.tensor_scalar(w_od[l], w_od[l].bitcast(I32), 1.0 / 7.5, -1.0, ALU.mult, ALU.add
                                   ).then_inc(w_unscaled, 1)
                if l == 0:
                    pool.wait_ge(w_sc, 16)
                pool.wait_ge(w_unscaled, l + 1)
                pool.tensor_tensor(w_od[l].rearrange("p (g e) -> p g e", e=GROUP),
                                   w_od[l].rearrange("p (g e) -> p g e", e=GROUP),
                                   sc[:, l].rearrange("p c g -> p (c g)").unsqueeze(2)
                                   .broadcast_to([P, NC * NG, GROUP]), ALU.mult).then_inc(w_scaled, 1)

            for h in range(2):
                ln1_root(0, h)
            for l in range(NL):
                dequantise(l)
            for h in range(2):
                for c in range(NC):
                    xt_lower(pool, 0, h, c)
            pool.wait_ge(wkvq_high, 2)
            pool.tensor_tensor(Wkvl[:], Wkv[:], Wkvh[:].bitcast(F32), ALU.subtract).then_inc(wkvq_split, 1)
            pool.tensor_tensor(Wql[:], Wqs[:], Wqh[:].bitcast(F32), ALU.subtract).then_inc(wkvq_split, 1)
            pool.wait_ge(w_row, 96)
            pool.wait_ge(consts, 5)

            def body(i, first, last):
                base_x(i, 0, first)
                add_squares(i, 0, 0)
                add_squares(i, 1, 0)
                ffn_root(i, 0, 0)
                ffn_root(i, 1, 0)
                base_x(i, 1, first)
                g_lower(pool, i, 0, 0, 0)
                g_lower(pool, i, 0, 0, 1)
                g_lower(pool, i, 1, 0, 0)
                base_xn(i, 0, first)
                h_lower(pool, i, 0, 0, 0)
                h_lower(pool, i, 0, 0, 1)
                h_lower(pool, i, 1, 0, 0)
                h_lower(pool, i, 1, 0, 1)
                add_squares(i, 0, 1)
                add_squares(i, 1, 1)
                ffn_root(i, 0, 1)
                if not last:
                    ln1_root(i + 1, 0)
                ffn_root(i, 1, 1)
                if not last:
                    ln1_root(i + 1, 1)
                g_lower(pool, i, 0, 1, 1)
                g_lower(pool, i, 1, 1, 0)
                g_lower(pool, i, 1, 1, 1)
                h_lower(pool, i, 0, 1, 1)
                add_squares(i, 0, 2)
                base_xn(i, 1, first)
                ffn_root(i, 0, 2)
                add_squares(i, 1, 2)
                ffn_root(i, 1, 2)
                ln2_root(i, 0)
                g_lower(pool, i, 0, 2, 0)
                ln2_root(i, 1)
                g_lower(pool, i, 0, 2, 1)
                g_lower(pool, i, 1, 2, 0)
                g_lower(pool, i, 1, 2, 1)
                ln2_root(i, 2)
                ln2_root(i, 3)

            batches(pool, body)

        @block.scalar
        def _(act):
            act.dma_start(lb[:], lora_b.rearrange("l (c p) r -> p l c r", p=P)).then_inc(w_lb, 16)
            act.dma_start(la_a.rearrange("r (l d) -> r l d", d=D), lora_a[0:4].rearrange("l r d -> r l d")
                          ).then_inc(w_la, 16)
            act.dma_start(la_b.rearrange("r (l d) -> r l d", d=D), lora_a[4:6].rearrange("l r d -> r l d")
                          ).then_inc(w_la, 16)
            for g, pair in enumerate((fw[:, 0], fw[:, 1], hT[0][:].rearrange("p (l n) -> p l n", l=2))):
                act.dma_start(pair.rearrange("p l (c d) -> p l c d", c=NC).bitcast(I32),
                              qweights[2 * g:2 * g + 2].rearrange("l (c p) d -> p l c d", p=P)).then_inc(w_q[g], 16)
                if g == 0:
                    act.dma_start(sc[:], scales.rearrange("l (c p) g -> p l c g", p=P)).then_inc(w_sc, 16)
            for w, dst in ((Wk, Wkv[:, :, 0:D]), (Wv, Wkv[:, :, D:]), (Wq, Wqs[:]), (Wo, Wos[:])):
                act.dma_start(dst, w.rearrange("(c p) n -> p c n", p=P)).then_inc(w_qkvo, 16)

            def xt_copy(b, h, c, last, ahead=False):
                r, n = (h * NC + c) % NROT, (h * NC + c) // NROT
                if not ahead:
                    r, n = rotating(b - 1, ("xt", h, c), last)
                    act.wait_ge(h_ready[h], nth(b - 1, NBLK * NC, c))
                act.wait_ge(rot_full[r], n + 1)
                act.activation(xTh[c][:, half(h)], RB[r][:], ACT.Copy).then_inc(xT_high, 1)
                act.activation(xT[c][:, half(h)], RB[r][:], ACT.Copy).then_inc(xT_ready, 1)

            def square(i, h, j, m):
                act.wait_ge(ffn_full[h][m], nth(i, 2 * NBLK, 2 * j))
                act.activation(fw[:, h, m, :], FB[h][m][:], ACT.Square, bias=b1c[:, j, m:m + 1]
                               ).then_inc(sq_ready[h], 1)

            def rb_copy(i, h, j, last):
                r, n = rotating(i, ("rs", h, j), last)
                act.wait_ge(rot_full[r], n + 1)
                act.activation(rb[:, h, :], RB[r][:], ACT.Copy).then_inc(rb_ready[h], 1)

            def gelu(i, h, j, m):
                act.wait_ge(yn_ready[h], nth(i, NBLK * NC, j * NC + m))
                act.activation(fw[:, h, m, :], fw[:, h, m, :], ACT.Gelu, bias=lnb[:, j, m:m + 1],
                               scale=lng[:, j, m:m + 1]).then_inc(g_ready[h], 1)

            def g_higher(i, h, j, m):
                act.wait_ge(g_ready[h], nth(i, NBLK * NC, j * NC + m))
                act.activation(gh[:, h, m, :], fw[:, h, m, :], ACT.Copy).then_inc(g_high[h], 1)

            def h_higher(i, h, j, m):
                act.wait_ge(h_ready[h], nth(i, NBLK * NC, j * NC + m))
                act.activation(hTh[m][:, half(h)], hT[m][:, half(h)], ACT.Copy).then_inc(h_high[h], 1)

            def k_exp(i, t):
                act.wait_ge(kv_ready, nth(i, NT, t))
                act.activation(E[:, t % HT, :], KV[:, t % HT, 0:D], ACT.Exp, bias=neg1[:, 0:1]).then_inc(e_ready, 1)

            def k_square(i, t):
                act.wait_ge(k_ready, nth(i, NT, t))
                act.activation(E[:, t % HT, :], K[:, t % HT, :], ACT.Square).then_inc(ks_ready, 1)

            def q_exp(i, h, m, last):
                r, n = rotating(i, ("q", h, m), last)
                act.wait_ge(rot_full[r], n + 1)
                if h:
                    act.wait_ge(q_ready, nth(i, 2 * NC, m))
                act.activation(eq[:, m, :], RB[r][:], ACT.Exp, bias=bqc[:, m:m + 1]).then_inc(eq_ready, 1)

            def m_copy(i):
                act.wait_ge(m_full, nth(i, 1, 0))
                act.activation(M[:].rearrange("p c d -> p (c d)"), AB[:], ACT.Copy).then_inc(m_ready, 1)

            for h in range(2):
                for c in range(NC):
                    xt_copy(0, h, c, False, ahead=True)

            def weights_high(l):
                if l >= 4:
                    act.wait_ge(wT_split, l - 3)
                if l % 2:
                    act.wait_ge(wT_full, l + 1)
                    act.activation(WT[l % 4].rearrange("p c d -> p (c d)"), bank[4][:], ACT.Copy).then_inc(wT_made, 1)
                else:
                    act.wait_ge(wmean_ready, l // 2 + 1)
                    for c in range(NC):
                        ins = act.activation(WT[l % 4][:, c, :], bank[1][:, c * D:(c + 1) * D], ACT.Identity,
                                             bias=wmean[:, 1, c:c + 1])
                    ins.then_inc(wT_made, 1)
                act.wait_ge(wT_made, l + 1)
                act.activation(WTh[:, l], WT[l % 4], ACT.Copy).then_inc(wT_high, 1)

            weights_high(0)
            weights_high(1)
            act.wait_ge(w_qkvo, 64)
            act.activation(Wkvh[:], Wkv[:], ACT.Copy).then_inc(wkvq_high, 1)
            act.activation(Wqh[:], Wqs[:], ACT.Copy).then_inc(wkvq_high, 1)
            for l in range(2, NL):
                weights_high(l)
            act.wait_ge(w_col, 64)
            act.wait_ge(vecs_ready, NBLK + 2)
            act.wait_ge(consts, 5)

            def body(i, first, last):
                square(i, 0, 0, 0)
                square(i, 0, 0, 1)
                square(i, 1, 0, 0)
                square(i, 1, 0, 1)
                k_exp(i, 0)
                k_exp(i, 1)
                rb_copy(i, 0, 0, last)
                k_square(i, 0)
                k_square(i, 1)
                gelu(i, 0, 0, 0)
                rb_copy(i, 1, 0, last)
                gelu(i, 0, 0, 1)
                g_higher(i, 0, 0, 0)
                g_higher(i, 0, 0, 1)
                gelu(i, 1, 0, 0)
                gelu(i, 1, 0, 1)
                g_higher(i, 1, 0, 0)
                g_higher(i, 1, 0, 1)
                k_exp(i, 2)
                k_exp(i, 3)
                h_higher(i, 0, 0, 0)
                k_square(i, 2)
                k_square(i, 3)
                h_higher(i, 0, 0, 1)
                h_higher(i, 1, 0, 0)
                h_higher(i, 1, 0, 1)
                square(i, 0, 1, 0)
                square(i, 0, 1, 1)
                square(i, 1, 1, 0)
                square(i, 1, 1, 1)
                k_exp(i, 4)
                k_exp(i, 5)
                k_square(i, 4)
                k_exp(i, 6)
                k_exp(i, 7)
                rb_copy(i, 0, 1, last)
                k_square(i, 5)
                k_square(i, 6)
                k_square(i, 7)
                gelu(i, 0, 1, 0)
                rb_copy(i, 1, 1, last)
                gelu(i, 0, 1, 1)
                g_higher(i, 0, 1, 0)
                g_higher(i, 0, 1, 1)
                gelu(i, 1, 1, 0)
                g_higher(i, 1, 1, 0)
                gelu(i, 1, 1, 1)
                g_higher(i, 1, 1, 1)
                q_exp(i, 0, 0, last)
                h_higher(i, 0, 1, 0)
                h_higher(i, 0, 1, 1)
                q_exp(i, 0, 1, last)
                q_exp(i, 1, 0, last)
                square(i, 0, 2, 0)
                square(i, 0, 2, 1)
                if not last:
                    xt_copy(i + 1, 0, 0, last)
                h_higher(i, 1, 1, 0)
                h_higher(i, 1, 1, 1)
                m_copy(i)
                q_exp(i, 1, 1, last)
                if not last:
                    xt_copy(i + 1, 0, 1, last)
                square(i, 1, 2, 0)
                rb_copy(i, 0, 2, last)
                square(i, 1, 2, 1)
                gelu(i, 0, 2, 0)
                if not last:
                    xt_copy(i + 1, 1, 0, last)
                g_higher(i, 0, 2, 0)
                rb_copy(i, 1, 2, last)
                gelu(i, 0, 2, 1)
                g_higher(i, 0, 2, 1)
                gelu(i, 1, 2, 0)
                g_higher(i, 1, 2, 0)
                gelu(i, 1, 2, 1)
                g_higher(i, 1, 2, 1)
                if not last:
                    xt_copy(i + 1, 1, 1, last)

            batches(act, body)

        @block.vector
        def _(dve):
            steps = [0]

            def chained(ins):
                ins.then_inc(dve_prep, 1)
                steps[0] += 1
                dve.wait_ge(dve_prep, steps[0])

            def ln1_statistics(b, h):
                dve.wait_ge(x_loaded[h], 16 * b + 16)
                for t in range(h * HT, (h + 1) * HT):
                    dve.bn_stats(st1[:, t, :], X[:, t, :]).then_inc(ln1_stats, 1)

            def ln1_mean_var(b, h):
                dve.wait_ge(ln1_stats, nth(b, NT, h * HT + HT - 1))
                dve.sem_inc(stats_seen)
                for t in range(h * HT, (h + 1) * HT):
                    dve.bn_aggr(mv1[:, t, :], st1[:, t, :]).then_inc(ln1_mean, 1)
                dve.wait_ge(ln1_mean, nth(b, NT, h * HT + HT - 1))
                dve.tensor_scalar(ve1[:, h * HT:(h + 1) * HT], mv1[:, h * HT:(h + 1) * HT, 1], EPS_LN, None, ALU.add
                                  ).then_inc(ln1_var, 1)

            def ln1_normalise(b, h, ahead=False):
                dve.wait_ge(ln1_rstd, nth(b, 2, h))
                if not ahead:
                    dve.wait_ge(xT_ready, nth(b - 1, 2 * NC, h * NC + NC - 1))
                    dve.wait_ge(xn_based, nth(b - 1, 2, h))
                for t in range(h * HT, (h + 1) * HT):
                    dve.tensor_scalar(XN[:, t, :], X[:, t, :], mv1[:, t, 0:1], rs1[:, t:t + 1],
                                      ALU.subtract, ALU.mult).then_inc(xn_ready, 1)

            def ffn_var(i, h, j, last):
                r, n = rotating(i, ("var", h, j), last)
                dve.wait_ge(rot_full[r], n + 1)
                dve.tensor_scalar(vef[:, h, :], RB[r][:].rearrange("p (t n) -> p t n", t=HT)[:, :, 0], EPS_LN, None,
                                  ALU.add).then_inc(fvar_ready[h], 1)

            def ffn_normalise(i, h, j, m):
                dve.wait_ge(rb_ready[h], nth(i, NBLK, j))
                dve.scalar_tensor_tensor(fw[:, h, m, :], FB[h][m][:], b1c[:, j, m:m + 1], rb[:, h, :],
                                         ALU.add, ALU.mult).then_inc(yn_ready[h], 1)

            def ffn_residual(i, h, j, m):
                dve.wait_ge(ffn_full[h][m], nth(i, 2 * NBLK, 2 * j + 1))
                before = xT[m] if j == 0 else hT[m]
                dve.scalar_tensor_tensor(hT[m][:, half(h)], FB[h][m][:], fb[:, 2 * j + 1, m:m + 1],
                                         before[:, half(h)], ALU.add, ALU.add).then_inc(h_ready[h], 1)

            def kv_bias(i, t, first, last):
                r, n = rotating(i, ("kv", t), last)
                dve.wait_ge(rot_full[r], n + 1)
                if t >= HT:
                    dve.wait_ge(kvt_done, nth(i, NT, t - HT))
                elif not first:
                    dve.wait_ge(kvt_done, nth(i - 1, NT, t + HT))
                dve.tensor_tensor(KV[:, t % HT, :], RB[r][:], kvb[:], ALU.add).then_inc(kv_ready, 1)

            def k_elu(i, t):
                dve.wait_ge(e_ready, nth(i, NT, t))
                dve.scalar_tensor_tensor(K[:, t % HT, :], E[:, t % HT, :], 1.0, KV[:, t % HT, 0:D],
                                         ALU.min, ALU.max).then_inc(k_ready, 1)

            def k_sum(i, t):
                dve.wait_ge(ks_ready, nth(i, NT, t))
                dve.tensor_reduce(ss[:, t % HT, :], E[:, t % HT, :].rearrange("p (h d) -> p h d", d=DEPTH),
                                  AX_X, ALU.add).then_inc(ss_ready, 1)

            def k_sum_eps(i, h):
                dve.wait_ge(ss_ready, nth(i, NT, h * HT + HT - 1))
                dve.tensor_scalar(sse[:], ss[:].rearrange("p t h -> p (t h)"), EPS_ATTN, None, ALU.add
                                  ).then_inc(sse_ready, 1)

            def k_rstd(i, h):
                dve.wait_ge(sse_ready, nth(i, 2, h))
                dve.tensor_scalar(guess[:].bitcast(I32), sse[:].bitcast(I32), -0.5, GUESS_BITS, ALU.mult, ALU.add
                                   ).then_inc(guess_ready, 1)
                for n in range(NEWTON):
                    step = h * NEWTON + n
                    dve.wait_ge(guess_ready, nth(i, 2 * NEWTON, step))
                    dve.tensor_tensor(guess_sq[:], guess[:], guess[:], ALU.mult).then_inc(guess_sq_ready, 1)
                    dve.wait_ge(guess_sq_ready, nth(i, 2 * NEWTON, step))
                    dve.scalar_tensor_tensor(guess_off[:], guess_sq[:], -0.5, sse[:], ALU.mult, ALU.mult
                                              ).then_inc(guess_off_ready, 1)
                    dve.wait_ge(guess_off_ready, nth(i, 2 * NEWTON, step))
                    if n < NEWTON - 1:
                        dve.scalar_tensor_tensor(guess[:], guess_off[:], 1.5, guess[:], ALU.add, ALU.mult
                                                  ).then_inc(guess_ready, 1)
                    else:
                        dve.scalar_tensor_tensor(rk[:].rearrange("p t h -> p (t h)"), guess_off[:], 1.5, guess[:],
                                                  ALU.add, ALU.mult).then_inc(rk_ready, 1)

            def k_hat(i, t):
                dve.wait_ge(rk_ready, nth(i, 2, t // HT))
                dve.tensor_tensor(K[:, t % HT, :].rearrange("p (h d) -> p h d", d=DEPTH),
                                  K[:, t % HT, :].rearrange("p (h d) -> p h d", d=DEPTH),
                                  rk[:, t % HT, :].unsqueeze(2).broadcast_to([P, NH, DEPTH]), ALU.mult
                                  ).then_inc(kh_ready, 1)

            def q_min(i, h, m):
                dve.wait_ge(eq_ready, nth(i, 2 * NC, h * NC + m))
                dve.tensor_scalar(eq[:, m, :], eq[:, m, :], 1.0, None, ALU.min).then_inc(eq_min, 1)

            def q_elu(i, h, m, last):
                r, n = rotating(i, ("q", h, m), last)
                dve.wait_ge(eq_min, nth(i, 2 * NC, h * NC + m))
                dve.scalar_tensor_tensor(qT[m][:, half(h)], RB[r][:], bq1[:, m:m + 1], eq[:, m, :],
                                         ALU.add, ALU.max).then_inc(q_ready, 1)

            def block_diagonal(i):
                dve.wait_ge(kvt_done, nth(i, NT, NT - 1))
                dve.tensor_tensor(BD[:].rearrange("p (c n) -> p c n", c=NC),
                                  AB[:, 0:NC * P].rearrange("p (c n) -> p c n", c=NC),
                                  head_mask[:].unsqueeze(1).broadcast_to([P, NC, P]), ALU.mult).then_inc(bd_ready, 1)

            def att_y(i, p, last):
                r, n = rotating(i, ("out", p), last)
                dve.wait_ge(rot_full[r], n + 1)
                dve.wait_ge(xn_based, nth(i, 2, p // 2))
                if p >= 2:
                    dve.wait_ge(res_ready, nth(i, NT, 2 * p - 3))
                dve.tensor_tensor(Y[:, p % 2].rearrange("p t d -> p (t d)"), RB[r][:],
                                  XNB[:, 2 * p:2 * p + 2, :].rearrange("p t d -> p (t d)"), ALU.add
                                  ).then_inc(y_ready, 1)
                dve.wait_ge(y_ready, nth(i, NT // 2, p))
                for t in range(2):
                    dve.bn_stats(st2[:, 2 * p + t, :], Y[:, p % 2, t, :]).then_inc(ln2_stats, 1)
                dve.wait_ge(ln2_stats, nth(i, NT, 2 * p + 1))
                dve.sem_inc(stats_seen)
                for t in range(2):
                    dve.bn_aggr(mv2[:, 2 * p + t, :], st2[:, 2 * p + t, :]).then_inc(ln2_mean, 1)
                dve.wait_ge(ln2_mean, nth(i, NT, 2 * p + 1))
                dve.tensor_scalar(ve2[:, 2 * p:2 * p + 2], mv2[:, 2 * p:2 * p + 2, 1], EPS_ATTN, None, ALU.add
                                  ).then_inc(ln2_var, 1)

            def att_result(i, p):
                dve.wait_ge(x_based, nth(i, 2, p // 2))
                for t in range(2):
                    dve.scalar_tensor_tensor(Y[:, p % 2, t, :], Y[:, p % 2, t, :], mv2[:, 2 * p + t, 0:1], gamma_r[:],
                                             ALU.subtract, ALU.mult).then_inc(z_ready, 1)
                dve.wait_ge(ln2_rstd, nth(i, NT // 2, p))
                for t in range(2):
                    n = 2 * p + t
                    dve.wait_ge(z_ready, nth(i, NT, n))
                    dve.scalar_tensor_tensor(RES[:, n, :], Y[:, p % 2, t, :], rs2[:, n:n + 1], RES[:, n, :],
                                             ALU.mult, ALU.add).then_inc(res_ready, 1)

            def finish(i, p, last):
                r, n = rotating(i, ("fin", p), last)
                dve.wait_ge(rot_full[r], n + 1)
                dve.wait_ge(res_ready, nth(i, NT, 2 * p + 1))
                pair = RES[:, 2 * p:2 * p + 2, :].rearrange("p t d -> p (t d)")
                dve.tensor_tensor(pair, RB[r][:], pair, ALU.add).then_inc(o_ready, 1)

            for h in range(2):
                ln1_statistics(0, h)
                ln1_mean_var(0, h)
            for h in range(2):
                ln1_normalise(0, h, ahead=True)

            dve.wait_ge(lbT_full, 1)
            for n in range(3):
                dve.tensor_copy(qT[n // 2][0:R, n % 2 * BANK:(n % 2 + 1) * BANK], bank[n][0:R, :]).then_inc(lbT_ready, 1)

            def add_lora(l):
                dve.wait_ge(w_scaled, l + 1)
                dve.wait_ge(lora_full, l + 1)
                dve.tensor_tensor(w_od[l], w_od[l], bank[2 + l % 2][:], ALU.add).then_inc(w_od_ready, 1)

            def weight_mean(l):
                if l:
                    dve.wait_ge(wT_made, l - 1)
                dve.wait_ge(wT_full, l + 1)
                chained(dve.tensor_reduce(wmean[:, 0, :], bank[1][:].rearrange("p (c d) -> p c d", c=NC), AX_X,
                                          ALU.add))
                dve.tensor_scalar(wmean[:, 1, :], wmean[:, 0, :], -1.0 / D, None, ALU.mult).then_inc(wmean_ready, 1)

            def weights_low(l):
                dve.wait_ge(wT_high, l + 1)
                dve.tensor_tensor(WTl[:, l], WT[l % 4], WTh[:, l].bitcast(F32), ALU.subtract).then_inc(wT_split, 1)

            for l in range(NL + 2):
                if l < NL:
                    add_lora(l)
                if l % 2 and l <= NL:
                    weight_mean(l - 1)
                if l >= 2:
                    weights_low(l - 2)

            dve.wait_ge(w_row, 96)
            dve.wait_ge(w_col, 64)
            dve.tensor_scalar(bq1[:], bqc[:], 1.0, None, ALU.add).then_inc(vecs_ready, 1)
            chained(dve.tensor_reduce(b1m[:], b1_r[:], AX_X, ALU.add))
            chained(dve.tensor_scalar(b1m[:], b1m[:], -1.0 / D, None, ALU.mult))
            for j in range(NBLK):
                dve.tensor_scalar(b1c[:, j, :], fb[:, 2 * j, :], b1m[:, j:j + 1], None, ALU.add
                                  ).then_inc(vecs_ready, 1)
            dve.tensor_scalar(kvb[:, 0:D], kvb[:, 0:D], 1.0, None, ALU.add).then_inc(vecs_ready, 1)
            dve.wait_ge(vecs_ready, NBLK + 2)
            dve.wait_ge(consts, 5)

            def body(i, first, last):
                kv_bias(i, 0, first, last)
                ffn_var(i, 0, 0, last)
                kv_bias(i, 1, first, last)
                ffn_var(i, 1, 0, last)
                k_elu(i, 0)
                k_elu(i, 1)
                ffn_normalise(i, 0, 0, 0)
                kv_bias(i, 2, first, last)
                ffn_normalise(i, 0, 0, 1)
                kv_bias(i, 3, first, last)
                if not last:
                    ln1_statistics(i + 1, 0)
                    ln1_mean_var(i + 1, 0)
                ffn_normalise(i, 1, 0, 0)
                ffn_normalise(i, 1, 0, 1)
                k_sum(i, 0)
                k_sum(i, 1)
                if not last:
                    ln1_statistics(i + 1, 1)
                    ln1_mean_var(i + 1, 1)
                g_lower(dve, i, 1, 0, 1)
                ffn_residual(i, 0, 0, 0)
                ffn_residual(i, 0, 0, 1)
                k_elu(i, 2)
                k_elu(i, 3)
                k_sum(i, 2)
                k_sum(i, 3)
                ffn_residual(i, 1, 0, 0)
                k_sum_eps(i, 0)
                ffn_residual(i, 1, 0, 1)
                k_rstd(i, 0)
                k_hat(i, 0)
                k_hat(i, 1)
                k_hat(i, 2)
                k_hat(i, 3)
                kv_bias(i, 4, first, last)
                kv_bias(i, 5, first, last)
                k_elu(i, 4)
                kv_bias(i, 6, first, last)
                k_elu(i, 5)
                ffn_var(i, 0, 1, last)
                kv_bias(i, 7, first, last)
                k_sum(i, 4)
                k_elu(i, 6)
                ffn_var(i, 1, 1, last)
                k_elu(i, 7)
                ffn_normalise(i, 0, 1, 0)
                k_sum(i, 5)
                ffn_normalise(i, 0, 1, 1)
                k_sum(i, 6)
                if not last:
                    ln1_normalise(i + 1, 0)
                k_sum(i, 7)
                k_sum_eps(i, 1)
                ffn_normalise(i, 1, 1, 0)
                ffn_normalise(i, 1, 1, 1)
                g_lower(dve, i, 0, 1, 0)
                k_rstd(i, 1)
                ffn_residual(i, 0, 1, 0)
                k_hat(i, 4)
                k_hat(i, 5)
                ffn_residual(i, 0, 1, 1)
                k_hat(i, 6)
                q_min(i, 0, 0)
                q_elu(i, 0, 0, last)
                q_min(i, 0, 1)
                h_lower(dve, i, 0, 1, 0)
                q_elu(i, 0, 1, last)
                k_hat(i, 7)
                q_min(i, 1, 0)
                block_diagonal(i)
                q_elu(i, 1, 0, last)
                ffn_residual(i, 1, 1, 0)
                ffn_residual(i, 1, 1, 1)
                if not last:
                    xt_lower(dve, i + 1, 0, 0)
                h_lower(dve, i, 1, 1, 1)
                ffn_var(i, 0, 2, last)
                q_min(i, 1, 1)
                h_lower(dve, i, 1, 1, 0)
                q_elu(i, 1, 1, last)
                if not last:
                    xt_lower(dve, i + 1, 0, 1)
                    ln1_normalise(i + 1, 1)
                ffn_normalise(i, 0, 2, 0)
                ffn_normalise(i, 0, 2, 1)
                att_y(i, 0, last)
                ffn_var(i, 1, 2, last)
                att_y(i, 1, last)
                att_result(i, 0)
                ffn_normalise(i, 1, 2, 0)
                ffn_normalise(i, 1, 2, 1)
                att_y(i, 2, last)
                ffn_residual(i, 0, 2, 0)
                ffn_residual(i, 0, 2, 1)
                att_result(i, 1)
                ffn_residual(i, 1, 2, 0)
                ffn_residual(i, 1, 2, 1)
                finish(i, 0, last)
                finish(i, 1, last)
                att_y(i, 3, last)
                if not last:
                    xt_lower(dve, i + 1, 1, 0)
                    xt_lower(dve, i + 1, 1, 1)
                att_result(i, 2)
                att_result(i, 3)
                finish(i, 2, last)
                finish(i, 3, last)

            batches(dve, body)

        @block.tensor
        def _(pe):
            def read_by(i, use):
                kind, *at = use
                return {
                    "var": lambda h, j: (fvar_ready[h], nth(i, NBLK, j)),
                    "rs": lambda h, j: (rb_ready[h], nth(i, NBLK, j)),
                    "kv": lambda t: (kv_ready, nth(i, NT, t)),
                    "q": lambda h, m: (q_ready, nth(i, 2 * NC, h * NC + m)),
                    "out": lambda p: (y_ready, nth(i, NT // 2, p)),
                    "xt": lambda h, c: (xT_ready, nth(i + 1, 2 * NC, h * NC + c)),
                    "fin": lambda p: (o_ready, nth(i, NT // 2, p)),
                }[kind](*at)

            def take(i, use, first, last):
                now = bank_uses(last)
                n = now.index(use)
                if n >= NROT:
                    before = read_by(i, now[n - NROT])
                elif first:
                    before = (xT_ready, AHEAD + n - NROT + 1)
                else:
                    before = read_by(i - 1, bank_uses(False)[n - NROT])
                pe.wait_ge(*before)
                return rotating(i, use, last)[0]

            def xt(b, h, c, last, ahead=False):
                if not ahead:
                    r = take(b - 1, ("xt", h, c), False, last)
                else:
                    r = (h * NC + c) % NROT
                    if h * NC + c >= NROT:
                        pe.wait_ge(xT_ready, h * NC + c - NROT + 1)
                pe.wait_ge(xn_ready, nth(b, NT, h * HT + HT - 1))
                for t in range(HT):
                    ins = pe.transpose(RB[r][:, t * P:(t + 1) * P], XN[:, h * HT + t, c * P:(c + 1) * P], ident[:])
                ins.then_inc(rot_full[r], 1)

            def high_products(l, h, k, high):
                for n, w in enumerate((WTl, WTh)):
                    for m in range(NC):
                        pe.matmul(FB[h][m][:], w[:, l, k, m * P:(m + 1) * P], high, start=(k == 0 and n == 0),
                                  stop=False)

            def low_products(l, h, k, low):
                for m in range(NC):
                    ins = pe.matmul(FB[h][m][:], WTh[:, l, k, m * P:(m + 1) * P], low, start=False,
                                    stop=(k == NC - 1))
                    if k == NC - 1:
                        ins.then_inc(ffn_full[h][m], 1)

            def first_linear(i, h, j, first):
                if first:
                    pe.wait_ge(wT_split, 2 * j + 1)
                if j == 0:
                    for k in range(NC):
                        pe.wait_ge(xT_high, nth(i, 2 * NC, h * NC + k))
                        high_products(0, h, k, xTh[k][:, half(h)])
                    for k in range(NC):
                        pe.wait_ge(xT_low, nth(i, 2 * NC, h * NC + k))
                        low_products(0, h, k, xTl[k][:, half(h)])
                else:
                    pe.wait_ge(h_ready[h], nth(i, NBLK * NC, j * NC - 1))
                    for k in range(NC):
                        pe.wait_ge(h_high[h], nth(i, (NBLK - 1) * NC, (j - 1) * NC + k))
                        high_products(2 * j, h, k, hTh[k][:, half(h)])
                    for k in range(NC):
                        pe.wait_ge(h_low[h][k], nth(i, NBLK - 1, j - 1))
                        low_products(2 * j, h, k, hTl[k][:, half(h)])

            def second_linear(i, h, j, first):
                if first:
                    pe.wait_ge(wT_split, 2 * j + 2)
                pe.wait_ge(yn_ready[h], nth(i, NBLK * NC, j * NC + NC - 1))
                for k in range(NC):
                    pe.wait_ge(g_high[h], nth(i, NBLK * NC, j * NC + k))
                    high_products(2 * j + 1, h, k, gh[:, h, k, :])
                for k in range(NC):
                    pe.wait_ge(g_low[h][k], nth(i, NBLK, j))
                    low_products(2 * j + 1, h, k, gl[:, h, k, :])

            def variance(i, h, j, first, last):
                r = take(i, ("var", h, j), first, last)
                pe.wait_ge(sqs_ready[h], nth(i, NBLK, j))
                for t in range(HT):
                    ins = pe.matmul(RB[r][:, t * P:(t + 1) * P], sqs[:, h, t * P:(t + 1) * P], mean_w[:],
                                    start=True, stop=True)
                ins.then_inc(rot_full[r], 1)

            def spread_rstd(i, h, j, first, last):
                r = take(i, ("rs", h, j), first, last)
                pe.wait_ge(frstd_ready[h], nth(i, NBLK, j))
                for t in range(HT):
                    ins = pe.transpose(RB[r][:, t * P:(t + 1) * P], rsf[:, h, t:t + 1].broadcast_to([P, P]), ident[:])
                ins.then_inc(rot_full[r], 1)

            def xt_parts_there(i, h):
                pe.wait_ge(xT_high, nth(i, 2 * NC, h * NC + NC - 1))
                pe.wait_ge(xT_low, nth(i, 2 * NC, h * NC + NC - 1))

            def project_kv(i, t, first, last):
                r = take(i, ("kv", t), first, last)
                if first and t == 0:
                    pe.wait_ge(wkvq_split, 2)
                if t % HT == 0:
                    xt_parts_there(i, t // HT)
                pairs = [(x, w, k) for x, w in ((xTh, Wkvl), (xTh, Wkvh), (xTl, Wkvh)) for k in range(NC)]
                for n, (x_, w, k) in enumerate(pairs):
                    ins = pe.matmul(RB[r][:], x_[k][:, t * P:(t + 1) * P], w[:, k, :],
                                    start=(n == 0), stop=(n == len(pairs) - 1))
                ins.then_inc(rot_full[r], 1)

            def add_vk(i, t, first):
                pe.wait_ge(kh_ready, nth(i, NT, t))
                if t == 0 and not first:
                    pe.wait_ge(m_ready, nth(i - 1, 1, 0))
                elif t == 0:
                    pe.wait_ge(wT_made, NL)
                for c in range(NC):
                    ins = pe.matmul(AB[:, c * P:(c + 1) * P], KV[:, t % HT, D + c * P:D + (c + 1) * P],
                                    K[:, t % HT, c * P:(c + 1) * P], start=(t == 0 and c == 0),
                                    stop=(t == NT - 1), skip_group_check=True)
                ins.then_inc(kvt_done, 1)

            def project_q(i, h, m, first, last):
                r = take(i, ("q", h, m), first, last)
                if m == 0:
                    xt_parts_there(i, h)
                pairs = [(w, x, k) for w, x in ((Wql, xTh), (Wqh, xTh), (Wqh, xTl)) for k in range(NC)]
                for n, (w, x_, k) in enumerate(pairs):
                    ins = pe.matmul(RB[r][:], w[:, k, m * P:(m + 1) * P], x_[k][:, half(h)],
                                    start=(n == 0), stop=(n == len(pairs) - 1))
                ins.then_inc(rot_full[r], 1)

            def make_m(i, first):
                if first:
                    pe.wait_ge(w_qkvo, 64)
                pe.wait_ge(bd_ready, nth(i, 1, 0))
                for c in range(NC):
                    ins = pe.matmul(AB[:, c * D:(c + 1) * D], BD[:, c * P:(c + 1) * P], Wos[:, c, :],
                                    start=True, stop=True)
                ins.then_inc(m_full, 1)

            def attend(i, p, first, last):
                r = take(i, ("out", p), first, last)
                pe.wait_ge(q_ready, nth(i, 2 * NC, p // 2 * NC + NC - 1))
                pe.wait_ge(m_ready, nth(i, 1, 0))
                for t in range(2):
                    for c in range(NC):
                        ins = pe.matmul(RB[r][:, t * D:(t + 1) * D], qT[c][:, (2 * p + t) * P:(2 * p + t + 1) * P],
                                        M[:, c, :], start=(c == 0), stop=(c == NC - 1))
                ins.then_inc(rot_full[r], 1)

            def to_rows(i, p, first, last):
                r = take(i, ("fin", p), first, last)
                pe.wait_ge(h_ready[p // 2], nth(i, NBLK * NC, NBLK * NC - 1))
                for t in range(2):
                    for c in range(NC):
                        ins = pe.transpose(RB[r][:, t * D + c * P:t * D + (c + 1) * P],
                                           hT[c][:, (2 * p + t) * P:(2 * p + t + 1) * P], ident[:])
                ins.then_inc(rot_full[r], 1)

            pe.wait_ge(consts, 5)
            pe.wait_ge(w_lb, 16)
            for n in range(NL * NC):
                ins = pe.transpose(bank[n // 4][0:R, n % 4 * P:(n % 4 + 1) * P], lb[:, n // NC, n % NC, :], ident[:])
            ins.then_inc(lbT_full, 1)
            for h in range(2):
                for c in range(NC):
                    xt(0, h, c, False, ahead=True)
            pe.wait_ge(w_la, 32)
            pe.wait_ge(lbT_ready, 3)
            for l in range(NL + 1):
                if l < NL:
                    if l >= 2:
                        pe.wait_ge(w_od_ready, l - 1)
                    for c in range(NC):
                        n = l * NC + c
                        ins = pe.matmul(bank[2 + l % 2][:, c * D:(c + 1) * D], lbT(n), la[l],
                                        start=True, stop=True)
                    ins.then_inc(lora_full, 1)
                if l >= 1:
                    m = l - 1
                    pe.wait_ge(w_od_ready, m + 1)
                    if m >= 2:
                        pe.wait_ge(wT_made, m - 1)
                    for k in range(NC):
                        for c in range(NC):
                            ins = pe.transpose(bank[(1, 4)[m % 2]][:, k * D + c * P:k * D + (c + 1) * P],
                                               w_od[m][:, c * D + k * P:c * D + (k + 1) * P], ident[:])
                    ins.then_inc(wT_full, 1)
            pe.wait_ge(wT_made, NL - 1)

            def body(i, first, last):
                first_linear(i, 0, 0, first)
                first_linear(i, 1, 0, first)
                project_kv(i, 0, first, last)
                variance(i, 0, 0, first, last)
                project_kv(i, 1, first, last)
                variance(i, 1, 0, first, last)
                spread_rstd(i, 0, 0, first, last)
                project_kv(i, 2, first, last)
                project_kv(i, 3, first, last)
                spread_rstd(i, 1, 0, first, last)
                project_kv(i, 4, first, last)
                project_kv(i, 5, first, last)
                project_kv(i, 6, first, last)
                second_linear(i, 0, 0, first)
                second_linear(i, 1, 0, first)
                first_linear(i, 0, 1, first)
                first_linear(i, 1, 1, first)
                add_vk(i, 0, first)
                add_vk(i, 1, first)
                add_vk(i, 2, first)
                add_vk(i, 3, first)
                variance(i, 0, 1, first, last)
                project_kv(i, 7, first, last)
                variance(i, 1, 1, first, last)
                spread_rstd(i, 0, 1, first, last)
                spread_rstd(i, 1, 1, first, last)
                project_q(i, 0, 0, first, last)
                project_q(i, 0, 1, first, last)
                project_q(i, 1, 0, first, last)
                second_linear(i, 0, 1, first)
                second_linear(i, 1, 1, first)
                add_vk(i, 4, first)
                add_vk(i, 5, first)
                add_vk(i, 6, first)
                first_linear(i, 0, 2, first)
                add_vk(i, 7, first)
                if not last:
                    xt(i + 1, 0, 0, last)
                project_q(i, 1, 1, first, last)
                make_m(i, first)
                variance(i, 0, 2, first, last)
                if not last:
                    xt(i + 1, 0, 1, last)
                first_linear(i, 1, 2, first)
                spread_rstd(i, 0, 2, first, last)
                attend(i, 0, first, last)
                attend(i, 1, first, last)
                variance(i, 1, 2, first, last)
                if not last:
                    xt(i + 1, 1, 0, last)
                spread_rstd(i, 1, 2, first, last)
                if not last:
                    xt(i + 1, 1, 1, last)
                attend(i, 2, first, last)
                second_linear(i, 0, 2, first)
                second_linear(i, 1, 2, first)
                to_rows(i, 0, first, last)
                to_rows(i, 1, first, last)
                attend(i, 3, first, last)
                to_rows(i, 2, first, last)
                to_rows(i, 3, first, last)

            batches(pe, body)


_INS = ["L0_attn_x", "L0_attn_Wq", "L0_attn_bq", "L0_attn_Wk", "L0_attn_bk", "L0_attn_Wv", "L0_attn_bv",
        "L0_attn_Wo", "L0_attn_bo", "L0_attn_gamma", "L0_attn_beta", "L0_ffn_qweights", "L0_ffn_scales",
        "L0_ffn_biases", "L0_ffn_lora_a", "L0_ffn_lora_b", "L0_ffn_ln_gamma", "L0_ffn_ln_beta"]
_OUTS = [((8, 1024, 256), "float32")]


def kernel(**inputs):
    import numpy as _np
    import concourse.bacc as _bacc
    from concourse import mybir as _mybir
    from concourse.bass_utils import run_bass_kernel_spmd as _run

    nc = _bacc.Bacc("TRN2", target_bir_lowering=False, num_devices=1)
    arrays, args = {}, []
    for name in _INS:
        a = _np.ascontiguousarray(inputs[name])
        arrays[f"in_{name}_dram"] = a
        args.append(nc.dram_tensor(f"in_{name}_dram", a.shape, _mybir.dt.from_np(a.dtype), kind="ExternalInput").ap())
    for i, (shape, dtype) in enumerate(_OUTS):
        dt = _mybir.dt.from_np(_np.dtype(dtype))
        args.append(nc.dram_tensor(f"out_{i}_dram", shape, dt, kind="ExternalOutput").ap())
    block_kernel(nc, *args)
    r = _run(nc, [arrays], core_ids=[0])
    got = tuple(r.results[0][f"out_{i}_dram"] for i in range(len(_OUTS)))
    return got[0]
```
